# Optimizing a Trainium2 kernel written in Bass

```python
import numpy as np
import jax
import jax.numpy as jnp

def _softmax(x, axis=-1):
    return jax.nn.softmax(x, axis=axis)
def _gelu(x):
    return jax.nn.gelu(x, approximate=True)
def _silu(x):
    return jax.nn.silu(x)
def _sigmoid(x):
    return jax.nn.sigmoid(x)
def _layernorm(x, axis=-1, eps=1e-5):
    m = jnp.mean(x, axis=axis, keepdims=True)
    v = jnp.var(x, axis=axis, keepdims=True)
    return (x - m) / jnp.sqrt(v + eps)
def _scatter_add(tgt, idx, src, axis=0):
    return tgt.at[idx].add(src)
def _segment_sum(src, seg, n):
    return jax.ops.segment_sum(src, seg, n)

kernel_name = 'mk_adj_preln_d4_adj_256_7150a2'

def setup_inputs(seed: int = 0):
    np.random.seed(seed)
    _w = jnp.asarray
    def _rec_inputs():
        import jax
        import jax.numpy as jnp
        _gk = jax.random.key(seed)
        x = -0.0005207 + 1.001 * jax.random.normal(jax.random.fold_in(_gk, 1), (32, 512, 256), jnp.float32)
        _w = (1.0 + jnp.arange(512, dtype=jnp.float32)) ** -0.5
        _w = _w / _w.mean()
        _pij = jnp.clip(0.015625 * _w[:, None] * _w[None, :], 0.0, 1.0)
        _a = jax.random.uniform(jax.random.fold_in(_gk, 2), (512, 512)) < _pij
        adj = _a.astype(jnp.int32)
        return x, adj
    x, adj = _rec_inputs()
    def _L0_gnn_setup():
        import jax, jax.numpy as jnp
        import numpy as np
        B, N, IN_F = (8, 1024, 256)
        N_H, D_F = (4, 64)
        NEG_SLOPE = 0.2
        key = jax.random.key(seed)
        k1, k2, k3, k4 = jax.random.split(key, 4)
        h = jax.random.normal(k1, (B, N, IN_F), dtype=jnp.float32)
        adj = jax.random.randint(k2, (N, N), 0, 2, dtype=jnp.int32)
        W = jax.random.normal(k3, (IN_F, N_H * D_F), dtype=jnp.float32) * IN_F ** (-0.5)
        a = jax.random.normal(k4, (N_H, 2 * D_F), dtype=jnp.float32) * D_F ** (-0.5)
        return {'h': h, 'adj': adj, 'W': W, 'a': a}
    _L0_gnn_all = _L0_gnn_setup()
    _L0_gnn_in = {k: v for k, v in _L0_gnn_all.items() if k in ('W', 'a', )}
    del _L0_gnn_all

    def _L1_gnn_setup():
        import jax, jax.numpy as jnp
        import numpy as np
        ALPHA = 0.2
        NEG_INF = -9000000000000000.0

        def _gat(inp, adj_mask, W, a):
            h = jnp.matmul(inp, W)
            F_ = h.shape[-1]
            f1 = jnp.matmul(h, a[:F_, 0])
            f2 = jnp.matmul(h, a[F_:, 0])
            e = jax.nn.leaky_relu(f1[:, :, None] + f2[:, None, :], ALPHA)
            if adj_mask is not None:
                e = jnp.where(adj_mask[None, :, :] > 0, e, NEG_INF)
            att = jax.nn.softmax(e, axis=2)
            h_prime = jnp.einsum('bij,bjf->bif', att, h)
            return jax.nn.elu(h_prime)
        key = jax.random.key(seed)
        ks = jax.random.split(key, 10)
        B, N, Fin, H, O = (16, 1024, 256, 512, 256)

        def xavier(k, shape):
            fan_in, fan_out = (shape[0], shape[-1])
            bound = 1.414 * np.sqrt(6.0 / (fan_in + fan_out))
            return jax.random.uniform(k, shape, jnp.float32, -bound, bound)
        return {'x': jax.random.normal(ks[0], (B, N, Fin), jnp.float32), 'adj': jax.random.randint(ks[1], (N, N), 0, 2, jnp.int32), 'mlp1_w': xavier(ks[2], (Fin, H)), 'mlp1_b': jnp.zeros((H,), jnp.float32), 'mlp2_w': xavier(ks[3], (H, O)), 'mlp2_b': jnp.zeros((O,), jnp.float32), 'W_fc': xavier(ks[4], (H, H)), 'a_fc': xavier(ks[5], (2 * H, 1)), 'W_hand': xavier(ks[6], (O, O)), 'a_hand': xavier(ks[7], (2 * O, 1))}
    _L1_gnn_all = _L1_gnn_setup()
    _L1_gnn_in = {k: v for k, v in _L1_gnn_all.items() if k in ('mlp1_w', 'mlp1_b', 'mlp2_w', 'mlp2_b', 'W_fc', 'a_fc', 'W_hand', 'a_hand', )}
    del _L1_gnn_all

    def _L2_gnn_setup():
        import jax, jax.numpy as jnp
        import numpy as np
        LEAKY_ALPHA = 0.2
        key = jax.random.key(seed)
        k1, k2, k3, k4 = jax.random.split(key, 4)
        B, N, Fin, Fout = (8, 2048, 256, 256)
        h = jax.random.normal(k1, (B, N, Fin), dtype=jnp.float32)
        adj = jax.random.randint(k2, (N, N), 0, 2, dtype=jnp.int32)
        W = jax.random.normal(k3, (Fin, Fout), dtype=jnp.float32) * (1.414 * (6.0 / (Fin + Fout)) ** 0.5)
        a = jax.random.normal(k4, (2 * Fout, 1), dtype=jnp.float32) * (1.414 * (6.0 / (2 * Fout + 1)) ** 0.5)
        return {'h': h, 'adj': adj, 'W': W, 'a': a}
    _L2_gnn_all = _L2_gnn_setup()
    _L2_gnn_in = {k: v for k, v in _L2_gnn_all.items() if k in ('W', 'a', )}
    del _L2_gnn_all

    def _L3_gnn_setup():
        import jax, jax.numpy as jnp
        import numpy as np
        IN_F = 256
        OUT_F = 256
        ALPHA = 0.01
        NEG_INF = -1000000000.0
        key = jax.random.key(seed)
        k_inp, k_adj, k_W, k_a = jax.random.split(key, 4)
        inp = jax.random.normal(k_inp, (8, 2048, IN_F), dtype=jnp.float32)
        adj = jax.random.randint(k_adj, (2048, 2048), 0, 2, dtype=jnp.int32)
        gain = 1.414
        lim_W = gain * np.sqrt(6.0 / (IN_F + OUT_F))
        W = jax.random.uniform(k_W, (IN_F, OUT_F), minval=-lim_W, maxval=lim_W, dtype=jnp.float32)
        lim_a = gain * np.sqrt(6.0 / (2 * OUT_F + 1))
        a = jax.random.uniform(k_a, (2 * OUT_F, 1), minval=-lim_a, maxval=lim_a, dtype=jnp.float32)
        return {'inp': inp, 'adj': adj, 'W': W, 'a': a}
    _L3_gnn_all = _L3_gnn_setup()
    _L3_gnn_in = {k: v for k, v in _L3_gnn_all.items() if k in ('W', 'a', )}
    del _L3_gnn_all

    return {
        "x": x,
        "adj": adj,
        "L0_gnn_W": _L0_gnn_in["W"],
        "L0_gnn_a": _L0_gnn_in["a"],
        "L1_gnn_mlp1_w": _L1_gnn_in["mlp1_w"],
        "L1_gnn_mlp1_b": _L1_gnn_in["mlp1_b"],
        "L1_gnn_mlp2_w": _L1_gnn_in["mlp2_w"],
        "L1_gnn_mlp2_b": _L1_gnn_in["mlp2_b"],
        "L1_gnn_W_fc": _L1_gnn_in["W_fc"],
        "L1_gnn_a_fc": _L1_gnn_in["a_fc"],
        "L1_gnn_W_hand": _L1_gnn_in["W_hand"],
        "L1_gnn_a_hand": _L1_gnn_in["a_hand"],
        "L2_gnn_W": _L2_gnn_in["W"],
        "L2_gnn_a": _L2_gnn_in["a"],
        "L3_gnn_W": _L3_gnn_in["W"],
        "L3_gnn_a": _L3_gnn_in["a"],
    }

def reference(x, adj, L0_gnn_W, L0_gnn_a, L1_gnn_mlp1_w, L1_gnn_mlp1_b, L1_gnn_mlp2_w, L1_gnn_mlp2_b, L1_gnn_W_fc, L1_gnn_a_fc, L1_gnn_W_hand, L1_gnn_a_hand, L2_gnn_W, L2_gnn_a, L3_gnn_W, L3_gnn_a):
    import jax
    import jax.numpy as jnp
    def _L0_gnn_ref(h, adj, W, a):
        import jax, jax.numpy as jnp
        import numpy as np
        B, N, IN_F = (8, 1024, 256)
        N_H, D_F = (4, 64)
        NEG_SLOPE = 0.2
        Wh = (h @ W).reshape(h.shape[0], h.shape[1], N_H, D_F)
        a_src, a_dst = (a[:, :D_F], a[:, D_F:])
        s_src = jnp.einsum('bnhd,hd->bnh', Wh, a_src)
        s_dst = jnp.einsum('bnhd,hd->bnh', Wh, a_dst)
        e = s_src[:, :, None, :] + s_dst[:, None, :, :]
        e = jnp.where(e > 0, e, NEG_SLOPE * e)
        mask = (adj != 0)[None, :, :, None]
        e = jnp.where(mask, e, -jnp.inf)
        alpha = jax.nn.softmax(e, axis=2)
        alpha = jnp.nan_to_num(alpha, nan=0.0)
        h_out = jnp.einsum('bijh,bjhd->bihd', alpha, Wh)
        h_out = h_out.reshape(h.shape[0], h.shape[1], N_H * D_F)
        return jax.nn.elu(h_out)

    def _L1_gnn_ref(x, adj, mlp1_w, mlp1_b, mlp2_w, mlp2_b, W_fc, a_fc, W_hand, a_hand):
        import jax, jax.numpy as jnp
        import numpy as np
        ALPHA = 0.2
        NEG_INF = -9000000000000000.0

        def _gat(inp, adj_mask, W, a):
            h = jnp.matmul(inp, W)
            F_ = h.shape[-1]
            f1 = jnp.matmul(h, a[:F_, 0])
            f2 = jnp.matmul(h, a[F_:, 0])
            e = jax.nn.leaky_relu(f1[:, :, None] + f2[:, None, :], ALPHA)
            if adj_mask is not None:
                e = jnp.where(adj_mask[None, :, :] > 0, e, NEG_INF)
            att = jax.nn.softmax(e, axis=2)
            h_prime = jnp.einsum('bij,bjf->bif', att, h)
            return jax.nn.elu(h_prime)
        out = jax.nn.relu(jnp.matmul(x, mlp1_w) + mlp1_b)
        residual = out
        out = _gat(jax.nn.relu(out), None, W_fc, a_fc)
        out = jax.nn.elu(out) + residual
        out = jax.nn.relu(jnp.matmul(out, mlp2_w) + mlp2_b)
        residual = out
        out = _gat(jax.nn.relu(out), adj, W_hand, a_hand)
        out = jax.nn.elu(out) + residual
        return jax.nn.relu(out)

    def _L2_gnn_ref(h, adj, W, a):
        import jax, jax.numpy as jnp
        import numpy as np
        LEAKY_ALPHA = 0.2
        Fout = W.shape[1]
        Wh = jnp.einsum('bnf,fo->bno', h, W)
        a1 = a[:Fout, 0]
        a2 = a[Fout:, 0]
        s_i = Wh @ a1
        s_j = Wh @ a2
        e = jax.nn.leaky_relu(s_i[:, :, None] + s_j[:, None, :], negative_slope=LEAKY_ALPHA)
        N = Wh.shape[1]
        mask = (adj > 0) | jnp.eye(N, dtype=bool)
        e = jnp.where(mask[None, :, :], e, -jnp.inf)
        attention = jax.nn.softmax(e, axis=-1)
        attention = jnp.nan_to_num(attention, nan=0.0)
        h_prime = jnp.einsum('bij,bjo->bio', attention, Wh)
        return jax.nn.elu(h_prime)

    def _L3_gnn_ref(inp, adj, W, a):
        import jax, jax.numpy as jnp
        import numpy as np
        IN_F = 256
        OUT_F = 256
        ALPHA = 0.01
        NEG_INF = -1000000000.0
        h = jnp.matmul(inp, W)
        a1 = a[:OUT_F, 0]
        a2 = a[OUT_F:, 0]
        e_src = jnp.einsum('bnf,f->bn', h, a1)
        e_dst = jnp.einsum('bnf,f->bn', h, a2)
        e = jax.nn.leaky_relu(e_src[:, :, None] + e_dst[:, None, :], negative_slope=ALPHA)
        e = jnp.where(adj[None, :, :] == 0, NEG_INF, e)
        attention = jax.nn.softmax(e, axis=-1)
        h_prime = jnp.matmul(attention, h)
        return jax.nn.relu(h_prime)

    h = jnp.maximum(_layernorm(x, axis=-1), 0.0)
    x = x + _L0_gnn_ref(h, adj, L0_gnn_W, L0_gnn_a)
    h = jnp.maximum(_layernorm(x, axis=-1), 0.0)
    x = x + _L1_gnn_ref(h, adj, L1_gnn_mlp1_w, L1_gnn_mlp1_b, L1_gnn_mlp2_w, L1_gnn_mlp2_b, L1_gnn_W_fc, L1_gnn_a_fc, L1_gnn_W_hand, L1_gnn_a_hand)
    h = jnp.maximum(_layernorm(x, axis=-1), 0.0)
    x = x + _L2_gnn_ref(h, adj, L2_gnn_W, L2_gnn_a)
    h = jnp.maximum(_layernorm(x, axis=-1), 0.0)
    x = x + _L3_gnn_ref(h, adj, L3_gnn_W, L3_gnn_a)
    return x


_drawn_inputs = setup_inputs


def setup_inputs(seed=0):
    import zlib

    import numpy as np

    out = dict(_drawn_inputs(seed))
    spreads = {'L1_gnn_mlp1_b': (0.0, 0.1), 'L1_gnn_mlp2_b': (0.0, 0.1)}
    factors = {'L1_gnn_a_hand': 3.073}
    for name, (base, spread) in spreads.items():
        noise = np.random.default_rng([zlib.crc32(name.encode()), seed]).standard_normal(out[name].shape)
        drawn = base * np.exp(spread * noise) if base else spread * noise
        out[name] = jnp.asarray(drawn.astype(out[name].dtype))
    for name, factor in factors.items():
        out[name] = (out[name] * factor).astype(out[name].dtype)
    return out
```

```python
from contextlib import ExitStack

import concourse.bass as bass
from concourse import mybir

ALU = mybir.AluOpType
ACT = mybir.ActivationFunctionType
F32 = mybir.dt.float32
F32R = mybir.dt.float32r
I32 = mybir.dt.int32
U8 = mybir.dt.uint8
AXX = mybir.AxisListType.X

B, N, F = 32, 512, 256
NBLK = 4
TINY = 1e-37
EPS = 1e-5
SHIFT = 30.0
STREAMS = 2


class Lanes:

    def __init__(self, nc, ctx):
        self.nc, self.ctx = nc, ctx
        self.q = {k: [] for k in ("pe", "dve", "act", "pool", "sp")}
        self.sems, self.count, self.seen = {}, {}, {}

    def emit(self, lane, fn, sig=None, by=1):
        if sig is None:
            self.q[lane].append((fn, None, 0))
            return None
        name = f"{lane}_{sig}"
        if name not in self.sems:
            self.sems[name] = self.ctx.enter_context(self.nc.semaphore(name))
            self.count[name] = 0
        self.count[name] += by
        self.q[lane].append((fn, self.sems[name], by))
        return (name, self.count[name])

    def wait(self, lane, *tokens):
        for name, value in tokens:
            if self.seen.get((lane, name), 0) < value:
                self.seen[(lane, name)] = value
                self.q[lane].append((None, self.sems[name], value))

    def play(self, lane, eng):
        for fn, sem, value in self.q[lane]:
            if fn is None:
                eng.wait_ge(sem, value)
            elif sem is None:
                fn(eng)
            else:
                fn(eng).then_inc(sem, value)


def build(nc, x_d, adj_d, L0_W, L0_a, m1_w, m1_b, m2_w, m2_b, fc_w, fc_a, ha_w, ha_a, L2_W, L2_a, L3_W, L3_a, out_d):
    ctx = ExitStack()
    with ctx:
        def sb(name, shape, dt=F32):
            return ctx.enter_context(nc.sbuf_tensor(name, shape, dt))

        L = Lanes(nc, ctx)
        emit, wait = L.emit, L.wait

        bank = [ctx.enter_context(nc.psum_tensor(f"bank{i}", [128, 512], F32)) for i in range(8)]
        bank_free = [() for _ in range(8)]
        turn = {"bank": 0, "Pf": 0}

        ident = sb("ident", [128, 128])
        kshift = sb("kshift", [128, 1])
        minus1 = sb("minus1", [128, 1])
        mhalf = sb("mhalf", [128, NBLK])
        maskT = {k: sb(f"mask_{k}", [128, NBLK, N], U8) for k in ("ne", "gt", "self")}
        empty = {k: sb(f"empty_{k}", [128, NBLK]) for k in ("ne", "gt")}
        b1 = sb("b1", [128, 4])
        b2 = sb("b2", [128, 2])

        def weights(name, kb, fo, nq):
            return {"hi": sb(name + "_hi", [128, kb, fo], F32R), "lo": sb(name + "_lo", [128, kb, fo], F32R),
                    "wa": sb(name + "_wa", [128, kb, 2 * nq], F32R) if nq else None,
                    "kb": kb, "fo": fo, "nq": nq}

        W0 = weights("w0", 2, 256, 8)
        WM1 = weights("wm1", 2, 512, 0)
        WFC = weights("wfc", 4, 512, 2)
        WM2 = weights("wm2", 4, 256, 0)
        WHA = weights("wha", 2, 256, 2)
        W2 = weights("w2", 2, 256, 2)
        W3 = weights("w3", 2, 256, 2)

        xs = [sb(f"x{s}", [128, NBLK, F]) for s in range(STREAMS)]
        XA = [sb(f"XA{s}", [128, 2, 512]) for s in range(STREAMS)]
        XB = [sb(f"XB{s}", [128, 2, 512]) for s in range(STREAMS)]
        identr = sb("identr", [128, 128], F32R)
        hT = [{p: sb(f"hT{s}{p}", [128, 2, N], F32R) for p in ("hi", "lo")} for s in range(STREAMS)]
        oT = [{p: sb(f"oT{s}{p}", [128, 4, N], F32R) for p in ("hi", "lo")} for s in range(STREAMS)]
        hws = [{p: sb(f"hw{i}{p}", [128, NBLK, 264], F32R) for p in ("hi", "lo")} for i in range(2)]
        hwf = {p: sb(f"hwf{p}", [128, NBLK, 512], F32R) for p in ("hi", "lo")}
        wdf = {p: sb(f"wdf{p}", [128, NBLK, 2], F32R) for p in ("hi", "lo")}
        P = [{p: sb(f"P{i}{p}", [128, NBLK, N], F32R) for p in ("hi", "lo")} for i in range(2)]
        Pf = [sb(f"Pf{i}", [128, 2, N]) for i in range(2)]
        ta, tb = XA[0], XB[0]
        rrow = sb("rrow", [128, N])
        sm = [{
            "st": sb(f"st{s}", [128, NBLK, 6]), "mv": sb(f"mv{s}", [128, NBLK, 2]),
            "ve": sb(f"ve{s}", [128, NBLK]), "rs": sb(f"rs{s}", [128, NBLK]),
            "sc": sb(f"sc{s}", [128, 8, NBLK]), "tm": sb(f"tm{s}", [128, 4]), "T": sb(f"T{s}", [128, 4]),
            "A": sb(f"A{s}", [128, 3, 4, NBLK]), "E": sb(f"E{s}", [128, 3, 4, NBLK]),
            "D": sb(f"D{s}", [128, 4, NBLK]), "rD": sb(f"rD{s}", [128, 4, NBLK]),
            "hs": sb(f"hs{s}", [128, 2]), "hsr": sb(f"hsr{s}", [128, 2, 2], F32R),
            "Sb": sb(f"Sb{s}", [128, F]),
        } for s in range(STREAMS)]

        P_free = [(), ()]
        Pf_free = [(), ()]
        hw_free = [(), ()]
        hwf_free = [()]
        tab_free = [()] * STREAMS
        rrow_free = [()]

        def take_bank():
            i = turn["bank"] % 8
            turn["bank"] += 1
            assert bank_free[i] is not None
            wait("pe", *bank_free[i])
            bank_free[i] = None
            return i

        def f32(ap):
            return ap.bitcast(F32)

        emit("pool", lambda e: e.memset(ident[:, :], 0.0), "c0")
        wait("pool", ("pool_c0", 1))
        t_id = emit("pool", lambda e: e.affine_select(out=ident[:, :], in_=ident[:, :], compare_op=ALU.not_equal,
                                                      fill=1.0, base=0, pattern=[[-1, 128]],
                                                      channel_multiplier=1), "id")
        emit("pool", lambda e: e.memset(kshift[:, :], SHIFT))
        emit("pool", lambda e: e.memset(minus1[:, :], -1.0))
        t_const = emit("pool", lambda e: e.memset(mhalf[:, :], -0.5), "const")

        adj_st = [Pf[0], Pf[1]]
        adj_v = adj_d.rearrange("(p b) j -> p b j", b=NBLK)
        t_adj = []
        for i in range(2):
            t_adj.append(emit("sp", lambda e, i=i: e.dma_start(adj_st[i][:, :, :].bitcast(I32),
                                                               adj_v[:, 2 * i:2 * i + 2, :]), f"adj{i}", 16))
        x_v = x_d.rearrange("n (p b) f -> n p b f", b=NBLK)
        o_v = out_d.rearrange("n (p b) f -> n p b f", b=NBLK)
        t_x = [None] * STREAMS
        t_store = [None] * STREAMS
        for s in range(STREAMS):
            t_x[s] = emit("sp", lambda e, s=s: e.dma_start(xs[s][:, :, :], x_v[s]), f"x{s}", 16)

        mrow = {"ne": ta, "gt": tb}
        last_ev = None
        for half in range(2):
            wait("dve", t_adj[half])
            src = adj_st[half][:, :, :].bitcast(I32)
            if last_ev:
                wait("dve", last_pe, last_e)
            t_m = {}
            for k, op in (("ne", ALU.not_equal), ("gt", ALU.is_gt)):
                t_m[k] = emit("dve", lambda e, k=k, op=op, src=src: e.tensor_scalar(
                    mrow[k][:, :, :], src, 0.0, None, op), "mrow")
            wait("dve", t_m["gt"])
            for k in ("ne", "gt"):
                last_e = emit("dve", lambda e, k=k, half=half: e.tensor_reduce(
                    empty[k][:, 2 * half:2 * half + 2], mrow[k][:, :, :], AXX, ALU.max), "emp")
            wait("pe", t_m["gt"], t_id)
            for k in ("ne", "gt"):
                for bj in range(NBLK):
                    bk = take_bank()
                    for b in range(2):
                        tp = emit("pe", lambda e, k=k, b=b, bj=bj, bk=bk: e.transpose(
                            bank[bk][:, b * 128:(b + 1) * 128], mrow[k][:, b, bj:N:NBLK], ident[:, :]), "mT")
                    last_pe = tp
                    wait("dve", tp)
                    last_ev = emit("dve", lambda e, k=k, bj=bj, bk=bk, half=half: e.tensor_copy(
                        maskT[k][:, bj, half * 256:(half + 1) * 256], bank[bk][:, 0:256]), "mTe")
                    bank_free[bk] = (last_ev,)
        wait("dve", last_e)
        for k in ("ne", "gt"):
            t_emp = emit("dve", lambda e, k=k: e.tensor_scalar(empty[k][:, :], empty[k][:, :], -1.0, 1.0,
                                                               ALU.mult, ALU.add), "emp2")
        wait("dve", last_ev, t_id)
        t_cp = emit("dve", lambda e: e.tensor_copy(maskT["self"][:, :, :], maskT["gt"][:, :, :]), "self")
        wait("dve", t_cp)
        for bj in range(NBLK):
            t_mask = emit("dve", lambda e, bj=bj: e.tensor_tensor(
                maskT["self"][:, bj, bj * 128:(bj + 1) * 128], maskT["self"][:, bj, bj * 128:(bj + 1) * 128],
                ident[:, :], ALU.max), "mask")

        t_bias = emit("sp", lambda e: e.dma_start(b1[:, :], m1_b.rearrange("(k p) -> p k", p=128),
                                                  allow_slow_non_contiguous=True), "b", 16)
        t_bias = emit("sp", lambda e: e.dma_start(b2[:, :], m2_b.rearrange("(k p) -> p k", p=128),
                                                  allow_slow_non_contiguous=True), "b", 16)

        stage = {"free": [], "n": 0}
        t_zero = None
        a_st = tb[:, 0, 0:32].rearrange("p (k q) -> p k q", q=8)

        def load_weights(w, w_d, a_fill):
            kb, fo, nq = w["kb"], w["fo"], w["nq"]
            wv = w_d.rearrange("(k p) n -> p k n", p=128)
            tiles = []
            per = 1024 // fo
            srcs = [Pf[0], Pf[1]]
            wait("sp", *stage["free"])
            toks = []
            for c in range((kb + per - 1) // per):
                k0, k1 = c * per, min(kb, (c + 1) * per)
                dst = srcs[c][:, :, :].rearrange("p a n -> p (a n)")[:, 0:(k1 - k0) * fo].rearrange(
                    "p (k n) -> p k n", n=fo)
                toks.append(emit("sp", lambda e, dst=dst, k0=k0, k1=k1: e.dma_start(dst, wv[:, k0:k1, :]),
                                 f"wl{c}", 16))
                tiles += [dst[:, k, :] for k in range(k1 - k0)]
            free = []
            wait("act", *toks)
            for k in range(kb):
                th = emit("act", lambda e, k=k: e.copy(w["hi"][:, k, :], tiles[k]), "whi")
            wait("dve", *toks, th)
            for k in range(kb):
                tl = emit("dve", lambda e, k=k: e.tensor_tensor(w["lo"][:, k, :], tiles[k], f32(w["hi"][:, k, :]),
                                                                ALU.subtract), "wlo")
            free.append(tl)
            if nq:
                ob = fo // 128
                if stage["n"]:
                    wait("dve", *stage["free"])
                tz = emit("dve", lambda e: e.memset(a_st, 0.0), "az")
                wait("sp", tz)
                ta_ = [a_fill(c) for c in range(1)][0]
                wait("pe", *toks, ta_)
                for k in range(kb):
                    bk = take_bank()
                    for o in range(ob):
                        tp = emit("pe", lambda e, k=k, o=o, bk=bk: e.transpose(
                            bank[bk][:, o * 128:(o + 1) * 128], tiles[k][:, o * 128:(o + 1) * 128],
                            ident[:, :]), "wT")
                    wait("dve", tp)
                    if stage.get("ta"):
                        wait("dve", stage["ta"])
                    te = emit("dve", lambda e, bk=bk, ob=ob: e.tensor_copy(
                        ta[:, 0, 0:ob * 128], bank[bk][:, 0:ob * 128]), "wTe")
                    bank_free[bk] = (te,)
                    wait("pe", te)
                    bk = take_bank()
                    for o in range(ob):
                        tp = emit("pe", lambda e, o=o, bk=bk, ob=ob: e.matmul(
                            bank[bk][:, 0:nq], ta[:, 0, o * 128:(o + 1) * 128], a_st[:, o, 0:nq],
                            start=(o == 0), stop=(o == ob - 1)), "wA")
                    stage["ta"] = tp
                    wait("dve", tp)
                    te = emit("dve", lambda e, k=k, bk=bk: e.tensor_copy(w["wa"][:, k, 0:nq], bank[bk][:, 0:nq]),
                              "wAh")
                    wait("dve", te)
                    te = emit("dve", lambda e, k=k, bk=bk: e.tensor_tensor(
                        w["wa"][:, k, nq:2 * nq], bank[bk][:, 0:nq], f32(w["wa"][:, k, 0:nq]), ALU.subtract), "wAl")
                    bank_free[bk] = (te,)
                free += [te, tp]
            stage["free"] = free
            stage["n"] += 1
            return [tl] + ([te] if nq else [])

        def fill_heads(_):
            for h in range(4):
                for t in range(2):
                    p0 = (h % 2) * 64
                    tok = emit("sp", lambda e, h=h, t=t, p0=p0: e.dma_start(
                        a_st[p0:p0 + 64, h // 2, t * 4 + h:t * 4 + h + 1],
                        L0_a[h, t * 64:(t + 1) * 64].rearrange("(p o) -> p o", o=1),
                        allow_slow_non_contiguous=True), "al", 16)
            return tok

        def fill_col(a_d, ob):
            def go(_):
                for t in range(2):
                    tok = emit("sp", lambda e, t=t: e.dma_start(
                        a_st[:, 0:ob, t], a_d[t * ob * 128:(t + 1) * ob * 128, 0].rearrange("(k p) -> p k", p=128),
                        allow_slow_non_contiguous=True), "al", 16)
                return tok
            return go

        stage["free"] = [last_pe, t_mask]
        t_w = {}
        t_w["L0"] = load_weights(W0, L0_W, fill_heads)
        t_w["m1"] = load_weights(WM1, m1_w, None)
        t_w["fc"] = load_weights(WFC, fc_w, fill_col(fc_a, 4))
        t_w["m2"] = load_weights(WM2, m2_w, None)
        t_w["ha"] = load_weights(WHA, ha_w, fill_col(ha_a, 2))
        t_w["L2"] = load_weights(W2, L2_W, fill_col(L2_a, 2))
        t_w["L3"] = load_weights(W3, L3_W, fill_col(L3_a, 2))
        Pf_free[0] = Pf_free[1] = tuple(stage["free"])
        tab_free[0] = tuple(stage["free"])
        t_idr = emit("dve", lambda e: e.tensor_copy(identr[:, :], ident[:, :]), "idr")
        wait("pe", t_idr)
        wait("act", t_const)
        wait("dve", t_mask, t_bias, t_emp)
        wait("act", t_emp)

        def mm3(out, a, b, first, last, sig=None, group=True):
            t = None
            for n, (u, v) in enumerate(((a[0], b[0]), (a[0], b[1]), (a[1], b[0]))):
                st, sp = first and n == 0, last and n == 2
                t = emit("pe", lambda e, u=u, v=v, st=st, sp=sp: e.matmul(
                    out, u, v, start=st, stop=sp, skip_group_check=not group),
                    sig if (sp and sig) else None) or t
            return t

        def layer_norm(s):
            m = sm[s]
            hn = XA[s][:, :, :].rearrange("p a (b n) -> p (a b) n", n=256)
            for b in range(NBLK):
                t = emit("dve", lambda e, b=b: e.bn_stats(m["st"][:, b, :], xs[s][:, b, :]), "st")
            wait("dve", t)
            for b in range(NBLK):
                t = emit("dve", lambda e, b=b: e.bn_aggr(m["mv"][:, b, :], m["st"][:, b, :]), "mv")
            wait("dve", t)
            t = emit("dve", lambda e: e.tensor_scalar(m["ve"][:, :], m["mv"][:, :, 1], EPS, None, ALU.add), "ve")
            wait("pool", t, t_const)
            t = emit("pool", lambda e: e.tensor_tensor(m["rs"][:, :], m["ve"][:, :], mhalf[:, :], ALU.pow), "rs")
            yield
            wait("dve", t, *tab_free[s])
            for b in range(NBLK):
                t = emit("dve", lambda e, b=b: e.tensor_scalar(
                    hn[:, b, :], xs[s][:, b, :], m["mv"][:, b, 0:1], m["rs"][:, b:b + 1],
                    ALU.subtract, ALU.mult), "hn")
            yield
            wait("pe", t)
            for k in range(2):
                bk = take_bank()
                for b in range(NBLK):
                    t = emit("pe", lambda e, b=b, k=k, bk=bk: e.transpose(
                        bank[bk][:, b * 128:(b + 1) * 128], hn[:, b, k * 128:(k + 1) * 128], ident[:, :]), "hT")
                wait("act", t)
                t = emit("act", lambda e, k=k, bk=bk: e.activation(
                    hT[s]["hi"][:, k, :], bank[bk][:, :], ACT.Relu, accum_out=m["hs"][:, k:k + 1]), "hThi")
                wait("dve", t)
                t = emit("dve", lambda e, k=k, bk=bk: e.scalar_tensor_tensor(
                    hT[s]["lo"][:, k, :], bank[bk][:, :], 0.0, f32(hT[s]["hi"][:, k, :]),
                    ALU.max, ALU.subtract), "hTlo")
                bank_free[bk] = (t,)
            return t

        def scores(s, src, w, t_src, alpha, nh):
            m, kb, nq = sm[s], w["kb"], w["nq"]
            wait("pe", t_src)
            bk = take_bank()
            for b in range(NBLK):
                for k in range(kb):
                    for n, p in enumerate(("hi", "lo")):
                        st = b == 0 and k == 0 and n == 0
                        last = b == NBLK - 1 and k == kb - 1 and n == 1
                        t = emit("pe", lambda e, b=b, k=k, p=p, st=st: e.matmul(
                            bank[bk][:, b * 2 * nq:(b + 1) * 2 * nq], src[p][:, k, b * 128:(b + 1) * 128],
                            w["wa"][:, k, :], start=st, stop=(k == kb - 1 and p == "lo"),
                            skip_group_check=True), "sc" if last else None)
            wait("dve", t)
            v = bank[bk][:, 0:NBLK * 2 * nq].rearrange("p (b c q) -> p q b c", b=NBLK, c=2)
            t = emit("dve", lambda e: e.tensor_reduce(m["sc"][:, 0:nq, :], v, AXX, ALU.add), "sc")
            bank_free[bk] = (t,)
            wait("dve", t)
            t = emit("dve", lambda e: e.tensor_reduce(m["tm"][:, 0:nh], m["sc"][:, nh:2 * nh, :], AXX, ALU.max),
                     "tm")
            yield
            wait("pe", t)
            bm = take_bank()
            for h in range(nh):
                t = emit("pe", lambda e, h=h: e.transpose(
                    bank[bm][:, h * 128:(h + 1) * 128], m["tm"][:, h:h + 1].broadcast_to([128, 128]),
                    ident[:, :]), "TM")
            wait("dve", t)
            v2 = bank[bm][:, 0:nh * 128].rearrange("p (h n) -> p h n", h=nh)
            t = emit("dve", lambda e: e.tensor_reduce(m["T"][:, 0:nh], v2, AXX, ALU.max), "T")
            bank_free[bm] = (t,)
            wait("dve", t)
            Tb = m["T"][:, 0:nh].rearrange("p (h o) -> p h o", o=1).broadcast_to([128, nh, NBLK])
            emit("dve", lambda e: e.tensor_tensor(m["A"][:, 0, 0:nh, :], m["sc"][:, nh:2 * nh, :], Tb,
                                                  ALU.subtract))
            t = emit("dve", lambda e: e.tensor_tensor(m["A"][:, 2, 0:nh, :], m["sc"][:, 0:nh, :], Tb, ALU.add),
                     "u")
            wait("dve", t)
            t = emit("dve", lambda e: e.tensor_scalar(m["A"][:, 1, 0:nh, :], m["A"][:, 0, 0:nh, :],
                                                      1.0 - alpha, None, ALU.mult), "u1")
            emit("dve", lambda e: e.tensor_scalar(m["A"][:, 2, 0:nh, :], m["A"][:, 2, 0:nh, :],
                                                  -(1.0 - alpha), 0.0, ALU.mult, ALU.min))
            wait("dve", t)
            t = emit("dve", lambda e: e.tensor_scalar(m["A"][:, 0, 0:nh, :], m["A"][:, 0, 0:nh, :],
                                                      alpha, None, ALU.mult), "u2")
            wait("act", t)
            t = emit("act", lambda e: e.activation(m["E"][:, :, 0:nh, :], m["A"][:, :, 0:nh, :], ACT.Exp,
                                                   bias=kshift[:, 0:1]), "E")
            yield
            return t

        def row_of(s, src, t_src):
            wait("pe", t_src)
            bk = take_bank()
            for b in range(NBLK):
                t = emit("pe", lambda e, b=b: e.transpose(
                    bank[bk][:, b * 128:(b + 1) * 128], src[:, b:b + 1].broadcast_to([128, 128]),
                    ident[:, :]), "row")
            return bk, t

        def build_P(s, h, mask, t_E):
            m = sm[s]
            bk, t_row = row_of(s, m["E"][:, 2, h, :], t_E)
            slot = s
            free, P_free[slot] = P_free[slot], None
            out = []
            for jp in range(2):
                f = turn["Pf"] % 2
                turn["Pf"] += 1
                wait("dve", t_row, t_E, *Pf_free[f])
                for jj in range(2):
                    j = 2 * jp + jj
                    r = m["E"][:, 1, h, j:j + 1]
                    if mask is None:
                        t = emit("dve", lambda e, jj=jj, r=r, f=f: e.tensor_scalar(
                            Pf[f][:, jj, :], bank[bk][:, :], r, None, ALU.max), "P")
                    else:
                        t = emit("dve", lambda e, jj=jj, j=j, r=r, f=f: e.scalar_tensor_tensor(
                            Pf[f][:, jj, :], bank[bk][:, :], r, mask[:, j, :], ALU.max, ALU.mult), "P")
                wait("act", t, *free)
                th = emit("act", lambda e, f=f, jp=jp: e.copy(P[slot]["hi"][:, 2 * jp:2 * jp + 2, :],
                                                              Pf[f][:, :, :]), "Phi")
                wait("pool", th, *free)
                tl = emit("pool", lambda e, f=f, jp=jp: e.tensor_tensor(
                    P[slot]["lo"][:, 2 * jp:2 * jp + 2, :], Pf[f][:, :, :],
                    f32(P[slot]["hi"][:, 2 * jp:2 * jp + 2, :]), ALU.subtract), "Plo")
                Pf_free[f] = (tl,)
                out.append(tl)
            bank_free[bk] = (t,)
            return slot, out

        def project(s, src, w, t_E, hw, width, free):
            m, kb = sm[s], w["kb"]
            for b in range(NBLK):
                bk = take_bank()
                for k in range(kb):
                    cols = slice(b * 128, (b + 1) * 128)
                    t = mm3(bank[bk][:, 0:width], (src["hi"][:, k, cols], src["lo"][:, k, cols]),
                            (w["hi"][:, k, :], w["lo"][:, k, :]), k == 0, k == kb - 1, "h")
                wj = m["E"][:, 0, 0, b:b + 1]
                wait("act", t, t_E, *free)
                t = emit("act", lambda e, b=b, bk=bk, wj=wj: e.activation(
                    hw["hi"][:, b, 0:width], bank[bk][:, 0:width], ACT.Copy, scale=wj), "hwhi")
                wait("dve", t, t_E, *free)
                t = emit("dve", lambda e, b=b, bk=bk, wj=wj: e.scalar_tensor_tensor(
                    hw["lo"][:, b, 0:width], bank[bk][:, 0:width], wj, f32(hw["hi"][:, b, 0:width]),
                    ALU.mult, ALU.subtract), "hwlo")
                bank_free[bk] = (t,)
            return t

        def weight_columns(src, hi, lo, t_E, free):
            wait("dve", t_E, *free)
            t = emit("dve", lambda e: e.tensor_copy(hi, src), "wch")
            wait("dve", t)
            return emit("dve", lambda e: e.tensor_tensor(lo, src, f32(hi), ALU.subtract), "wcl")

        def attend(s, hw, slot, t_P, t_hw):
            banks = []
            wait("pe", *t_hw)
            for i in range(NBLK):
                bk = take_bank()
                cols = slice(i * 128, (i + 1) * 128)
                for j in range(NBLK):
                    wait("pe", t_P[j // 2])
                    t = mm3(bank[bk][:, 0:258], (P[slot]["hi"][:, j, cols], P[slot]["lo"][:, j, cols]),
                            (hw["hi"][:, j, 0:258], hw["lo"][:, j, 0:258]), j == 0, j == NBLK - 1, "att")
                banks.append((bk, t))
            P_free[slot] = (t,)
            return banks, t

        def row_sum_inverse(s, bk, i, t):
            m = sm[s]
            wait("dve", t)
            t = emit("dve", lambda e: e.tensor_scalar(m["D"][:, 0, i:i + 1], bank[bk][:, 256:257], TINY, None,
                                                      ALU.max), "D")
            wait("dve", t)
            return emit("dve", lambda e: e.reciprocal(m["rD"][:, 0, i:i + 1], m["D"][:, 0, i:i + 1]), "rD")

        def column_sums(s, w, t_hs):
            m = sm[s]
            wait("dve", t_hs)
            t = emit("dve", lambda e: e.tensor_copy(m["hsr"][:, :, 0], m["hs"][:, :]), "hs")
            wait("dve", t)
            t = emit("dve", lambda e: e.tensor_tensor(m["hsr"][:, :, 1], m["hs"][:, :], f32(m["hsr"][:, :, 0]),
                                                      ALU.subtract), "hs")
            wait("pe", t)
            bk = take_bank()
            for k in range(2):
                a = tuple(m["hsr"][:, k, p:p + 1].broadcast_to([128, 128]) for p in range(2))
                t = mm3(bank[bk][:, 0:256], a, (w["hi"][:, k, :], w["lo"][:, k, :]), k == 0, k == 1, "S")
            wait("act", t)
            t = emit("act", lambda e: e.activation(m["Sb"][:, :], bank[bk][:, 0:256], ACT.Copy, scale=1.0 / N),
                     "Sb")
            bank_free[bk] = (t,)
            return t

        def gat256(s, src, w, t_src, alpha, mask):
            m = sm[s]
            t_E = yield from scores(s, src, w, t_src, alpha, 1)
            hwi = s
            hw, free = hws[hwi], hw_free[hwi]
            hw_free[hwi] = None
            slot, t_P = build_P(s, 0, mask, t_E)
            yield
            wc = m["E"][:, 0, 0, :].rearrange("p (b o) -> p b o", o=1).broadcast_to([128, NBLK, 2])
            t_c = weight_columns(wc, hw["hi"][:, :, 256:258], hw["lo"][:, :, 256:258], t_E, free)
            t_h = project(s, src, w, t_E, hw, 256, free)
            yield
            banks, t = attend(s, hw, slot, t_P, (t_h, t_c))
            hw_free[hwi] = (t,)
            return banks

        def batch(b):
            s = b % STREAMS
            m = sm[s]
            x = xs[s]
            ta, tb = XA[s], XB[s]
            tA = ta[:, :, :].rearrange("p a (b n) -> p (a b) n", n=256)
            tB = tb[:, :, :].rearrange("p a (b n) -> p (a b) n", n=256)

            wait("dve", t_x[s])
            t_h = yield from layer_norm(s)
            yield
            wait("pe", *t_w["L0"])
            t_E = yield from scores(s, hT[s], W0, t_h, 0.2, 4)
            hwi = s
            hw, free = hws[hwi], hw_free[hwi]
            hw_free[hwi] = None
            hv = {p: hw[p][:, :, :].rearrange("p b (h n) -> p b h n", n=66) for p in ("hi", "lo")}
            Pn = build_P(s, 0, maskT["ne"], t_E)
            yield
            for bl in range(NBLK):
                wc = m["E"][:, 0, :, bl:bl + 1].broadcast_to([128, 4, 2])
                t_c = weight_columns(wc, hv["hi"][:, bl, :, 64:66], hv["lo"][:, bl, :, 64:66], t_E, free)
            for bl in range(NBLK):
                bk = take_bank()
                cols = slice(bl * 128, (bl + 1) * 128)
                for k in range(2):
                    t = mm3(bank[bk][:, 0:256], (hT[s]["hi"][:, k, cols], hT[s]["lo"][:, k, cols]),
                            (W0["hi"][:, k, :], W0["lo"][:, k, :]), k == 0, k == 1, "h")
                wait("dve", t, *tab_free[s])
                wb = m["E"][:, 0, :, bl:bl + 1].broadcast_to([128, 4, 64])
                t = emit("dve", lambda e, bk=bk, wb=wb, bl=bl: e.tensor_tensor(
                    tA[:, bl, :].rearrange("p (h n) -> p h n", n=64),
                    bank[bk][:, 0:256].rearrange("p (h n) -> p h n", n=64), wb, ALU.mult), "hwf")
                bank_free[bk] = (t,)
                wait("act", t, *free)
                t = emit("act", lambda e, bl=bl: e.copy(
                    hv["hi"][:, bl, :, 0:64], tA[:, bl, :].rearrange("p (h n) -> p h n", n=64)), "hwhi0")
                wait("pool", t, *free)
                t_hw = emit("pool", lambda e, bl=bl: e.tensor_tensor(
                    hv["lo"][:, bl, :, 0:64], tA[:, bl, :].rearrange("p (h n) -> p h n", n=64),
                    f32(hv["hi"][:, bl, :, 0:64]), ALU.subtract), "hwlo0")
            tab_free[s] = (t_hw,)
            yield
            wait("pe", t_hw, t_c)
            for h in range(4):
                slot, t_P = Pn
                bk = take_bank()
                for i in range(NBLK):
                    cols = slice(i * 128, (i + 1) * 128)
                    for j in range(NBLK):
                        wait("pe", t_P[j // 2])
                        t = mm3(bank[bk][:, i * 66:(i + 1) * 66],
                                (P[slot]["hi"][:, j, cols], P[slot]["lo"][:, j, cols]),
                                (hv["hi"][:, j, h, :], hv["lo"][:, j, h, :]),
                                i == 0 and j == 0, j == NBLK - 1, "att0" if i == 3 else None, group=False)
                P_free[slot] = (t,)
                t_att = t
                if h < 3:
                    Pn = build_P(s, h + 1, maskT["ne"], t_E)
                yield
                t = t_att
                ov = bank[bk][:, 0:264].rearrange("p (i n) -> p i n", n=66)
                wait("dve", t)
                t = emit("dve", lambda e, ov=ov, h=h: e.tensor_scalar(m["D"][:, h, :], ov[:, :, 64], TINY, None,
                                                                      ALU.max), "D")
                wait("dve", t)
                t = emit("dve", lambda e, h=h: e.reciprocal(m["rD"][:, h, :], m["D"][:, h, :]), "rD")
                wait("dve", t, *tab_free[s])
                rb = m["rD"][:, h, :].rearrange("p (i o) -> p i o", o=1).broadcast_to([128, NBLK, 64])
                y = ta[:, 0, 0:256].rearrange("p (i n) -> p i n", n=64)
                ex = tb[:, 0, 0:256].rearrange("p (i n) -> p i n", n=64)
                xh = x[:, :, h * 64:(h + 1) * 64]
                t = emit("dve", lambda e, y=y, ov=ov, rb=rb: e.tensor_tensor(y, ov[:, :, 0:64], rb, ALU.mult),
                         "y0")
                bank_free[bk] = (t,)
                wait("act", t, *tab_free[s])
                te = emit("act", lambda e, y=y, ex=ex: e.activation(ex, y, ACT.Exp), "e0")
                wait("dve", t)
                t = emit("dve", lambda e, y=y, xh=xh: e.scalar_tensor_tensor(xh, y, 0.0, xh, ALU.max, ALU.add),
                         "x0")
                wait("dve", te)
                t2 = emit("dve", lambda e, ex=ex: e.tensor_scalar(ex, ex, 1.0, -1.0, ALU.min, ALU.add), "m0")
                wait("dve", t, t2)
                t = emit("dve", lambda e, ex=ex, xh=xh: e.tensor_tensor(xh, xh, ex, ALU.add), "x0b")
                tab_free[s] = (t,)
            hw_free[hwi] = (t_att,)
            wait("dve", t)
            yield

            t_h = yield from layer_norm(s)
            yield
            wait("pe", t_h, *t_w["m1"])
            o = oT[s]
            for fo in range(4):
                bk = take_bank()
                cols = slice(fo * 128, (fo + 1) * 128)
                for k in range(2):
                    t = mm3(bank[bk][:, :], (WM1["hi"][:, k, cols], WM1["lo"][:, k, cols]),
                            (hT[s]["hi"][:, k, :], hT[s]["lo"][:, k, :]), k == 0, k == 1, "m1")
                wait("dve", t, *tab_free[s])
                t = emit("dve", lambda e, bk=bk, fo=fo: e.tensor_scalar(
                    ta[:, fo % 2, :], bank[bk][:, :], b1[:, fo:fo + 1], 0.0, ALU.add, ALU.max), "m1")
                bank_free[bk] = (t,)
                wait("act", t)
                t = emit("act", lambda e, fo=fo: e.copy(o["hi"][:, fo, :], ta[:, fo % 2, :]), "o1hi")
                wait("pool", t)
                t_o = emit("pool", lambda e, fo=fo: e.tensor_tensor(
                    o["lo"][:, fo, :], ta[:, fo % 2, :], f32(o["hi"][:, fo, :]), ALU.subtract), "o1lo")
                if fo == 1:
                    tab_free[s] = (t_o,)
            tab_free[s] = (t_o,)
            yield
            wait("pe", *t_w["fc"])
            t_E = yield from scores(s, o, WFC, t_o, 0.2, 1)
            slot, t_P = build_P(s, 0, None, t_E)
            yield
            free = hwf_free[0]
            hwf_free[0] = None
            wc = m["E"][:, 0, 0, :].rearrange("p (b o) -> p b o", o=1).broadcast_to([128, NBLK, 2])
            t_c = weight_columns(wc, wdf["hi"][:, :, :], wdf["lo"][:, :, :], t_E, free)
            t_hw = project(s, o, WFC, t_E, hwf, 512, free)
            yield
            wait("pe", t_hw, t_c, *t_P)
            bk = take_bank()
            for i in range(NBLK):
                cols = slice(i * 128, (i + 1) * 128)
                for j in range(NBLK):
                    t = mm3(bank[bk][:, 2 * i:2 * i + 2], (P[slot]["hi"][:, j, cols], P[slot]["lo"][:, j, cols]),
                            (wdf["hi"][:, j, :], wdf["lo"][:, j, :]), i == 0 and j == 0, j == NBLK - 1,
                            "D" if i == 3 else None, group=False)
            wait("dve", t)
            t = emit("dve", lambda e, bk=bk: e.reciprocal(
                m["rD"][:, 0, :], bank[bk][:, 0:8].rearrange("p (i o) -> p i o", o=2)[:, :, 0]), "rD")
            bank_free[bk] = (t,)
            obanks = []

            def attend_f(fo):
                bk = take_bank()
                fc = slice(fo * 128, (fo + 1) * 128)
                for j in range(NBLK):
                    tt = mm3(bank[bk][:, :], (hwf["hi"][:, j, fc], hwf["lo"][:, j, fc]),
                             (P[slot]["hi"][:, j, :], P[slot]["lo"][:, j, :]), j == 0, j == NBLK - 1, "attf")
                return bk, tt

            obanks.append(attend_f(0))
            bk, t = row_of(s, m["rD"][:, 0, :], t)
            wait("act", t, *rrow_free[0])
            t_rr = emit("act", lambda e, bk=bk: e.copy(rrow[:, :], bank[bk][:, :]), "rrow")
            bank_free[bk] = (t_rr,)
            obanks.append(attend_f(1))
            for half in range(2):
                if half == 1:
                    obanks.append(attend_f(2))
                    obanks.append(attend_f(3))
                    P_free[slot] = (obanks[3][1],)
                    hwf_free[0] = (obanks[3][1],)
                wait("dve", t_rr, *tab_free[s])
                for q in range(2):
                    bk, t = obanks[2 * half + q]
                    wait("dve", t)
                    t = emit("dve", lambda e, q=q, bk=bk: e.tensor_tensor(
                        ta[:, q, :], bank[bk][:, :], rrow[:, :], ALU.mult), "yf")
                    bank_free[bk] = (t,)
                rrow_free[0] = (t,)
                wait("act", t, *tab_free[s])
                t = emit("act", lambda e: e.activation(tb[:, :, :], ta[:, :, :], ACT.Exp), "ef")
                yield
                wait("dve", t)
                t = emit("dve", lambda e: e.tensor_scalar(tb[:, :, :], tb[:, :, :], 1.0, None, ALU.min), "mf")
                wait("act", t)
                t = emit("act", lambda e: e.activation(tb[:, :, :], tb[:, :, :], ACT.Exp, bias=minus1[:, 0:1]),
                         "ef2")
                wait("dve", t)
                t = emit("dve", lambda e: e.scalar_tensor_tensor(
                    ta[:, :, :], ta[:, :, :], 0.0, tb[:, :, :], ALU.max, ALU.add), "gf")
                hs_ = slice(2 * half, 2 * half + 2)
                wait("pool", t)
                t2 = emit("pool", lambda e, hs_=hs_: e.tensor_tensor(
                    tb[:, :, :], f32(o["hi"][:, hs_, :]), f32(o["lo"][:, hs_, :]), ALU.add), "resf")
                wait("dve", t, t2)
                t = emit("dve", lambda e: e.scalar_tensor_tensor(
                    ta[:, :, :], ta[:, :, :], -1.0, tb[:, :, :], ALU.add, ALU.add), "o2")
                wait("act", t)
                t = emit("act", lambda e, hs_=hs_: e.copy(o["hi"][:, hs_, :], ta[:, :, :]), "o2hi")
                wait("pool", t)
                t_o = emit("pool", lambda e, hs_=hs_: e.tensor_tensor(
                    o["lo"][:, hs_, :], ta[:, :, :], f32(o["hi"][:, hs_, :]), ALU.subtract), "o2lo")
                tab_free[s] = (t_o,)
                yield
            wait("pe", t_o, *t_w["m2"])
            o3 = ta
            for fo in range(2):
                bk = take_bank()
                cols = slice(fo * 128, (fo + 1) * 128)
                for k in range(4):
                    t = mm3(bank[bk][:, :], (WM2["hi"][:, k, cols], WM2["lo"][:, k, cols]),
                            (o["hi"][:, k, :], o["lo"][:, k, :]), k == 0, k == 3, "m2")
                wait("dve", t, *tab_free[s])
                t3 = emit("dve", lambda e, bk=bk, fo=fo: e.tensor_scalar(
                    o3[:, fo, :], bank[bk][:, :], b2[:, fo:fo + 1], 0.0, ALU.add, ALU.max), "m2")
                bank_free[bk] = (t3,)
                wait("act", t3)
                t_hs = emit("act", lambda e, fo=fo: e.activation(
                    hT[s]["hi"][:, fo, :], o3[:, fo, :], ACT.Copy, accum_out=m["hs"][:, fo:fo + 1]), "o3hi")
                wait("pool", t_hs)
                t_o = emit("pool", lambda e, fo=fo: e.tensor_tensor(
                    hT[s]["lo"][:, fo, :], o3[:, fo, :], f32(hT[s]["hi"][:, fo, :]), ALU.subtract), "o3lo")
            yield
            tab_free[s] = (t_o,)
            t_S = column_sums(s, WHA, t_hs)
            yield
            wait("pe", *t_w["ha"])
            banks = yield from gat256(s, hT[s], WHA, t_o, 0.2, maskT["gt"])
            for i, (bk, t) in enumerate(banks):
                t = row_sum_inverse(s, bk, i, t)
                wait("act", t, *tab_free[s])
                t = emit("act", lambda e, i=i, bk=bk: e.activation(
                    tA[:, i, :], bank[bk][:, 0:256], ACT.Copy, scale=m["rD"][:, 0, i:i + 1]), "yh")
                bank_free[bk] = (t,)
            rbanks = []
            for bp in range(2):
                bk = take_bank()
                for bb in range(2):
                    for k in range(2):
                        out = bank[bk][:, bb * 256 + k * 128:bb * 256 + (k + 1) * 128]
                        cols = slice((2 * bp + bb) * 128, (2 * bp + bb + 1) * 128)
                        for p in ("hi", "lo"):
                            tr = emit("pe", lambda e, out=out, k=k, cols=cols, p=p, st=(bb == 0 and k == 0 and p == "hi"):
                                      e.matmul(out, hT[s][p][:, k, cols], identr[:, :], start=st, stop=(p == "lo"),
                                               skip_group_check=True), "r3" if (bb, k, p) == (1, 1, "lo") else None)
                rbanks.append((bk, tr))
            wait("dve", t, t_S)
            for i in range(NBLK):
                t = emit("dve", lambda e, i=i: e.scalar_tensor_tensor(
                    tA[:, i, :], m["Sb"][:, :], empty["gt"][:, i:i + 1], tA[:, i, :], ALU.mult, ALU.add), "yh2")
            wait("act", t)
            t = emit("act", lambda e: e.activation(tb[:, :, :], ta[:, :, :], ACT.Exp), "eh")
            yield
            wait("dve", t)
            t = emit("dve", lambda e: e.tensor_scalar(tb[:, :, :], tb[:, :, :], 1.0, None, ALU.min), "mh")
            wait("act", t)
            t = emit("act", lambda e: e.activation(tb[:, :, :], tb[:, :, :], ACT.Exp, bias=minus1[:, 0:1]), "eh2")
            wait("dve", t)
            t = emit("dve", lambda e: e.scalar_tensor_tensor(
                ta[:, :, :], ta[:, :, :], 0.0, tb[:, :, :], ALU.max, ALU.add), "gh")
            wait("dve", t)
            for bp in range(2):
                bk, t_r = rbanks[bp]
                wait("dve", t_r)
                t = emit("dve", lambda e, bp=bp, bk=bk: e.scalar_tensor_tensor(
                    ta[:, bp, :], ta[:, bp, :], -1.0, bank[bk][:, :], ALU.add, ALU.add), "gh2")
                bank_free[bk] = (t,)
            wait("dve", t)
            t = emit("dve", lambda e: e.scalar_tensor_tensor(
                x[:, :, :], tA, 0.0, x[:, :, :], ALU.max, ALU.add), "xh")
            tab_free[s] = (t,)
            wait("dve", t)
            yield

            t_h = yield from layer_norm(s)
            yield
            wait("pe", *t_w["L2"])
            banks = yield from gat256(s, hT[s], W2, t_h, 0.2, maskT["self"])
            for i, (bk, t) in enumerate(banks):
                t = row_sum_inverse(s, bk, i, t)
                wait("dve", t, *tab_free[s])
                t = emit("dve", lambda e, i=i, bk=bk: e.tensor_scalar(
                    tA[:, i, :], bank[bk][:, 0:256], m["rD"][:, 0, i:i + 1], 0.0, ALU.mult, ALU.max), "rl2")
                wait("act", t, *tab_free[s])
                t = emit("act", lambda e, i=i, bk=bk: e.activation(
                    tB[:, i, :], bank[bk][:, 0:256], ACT.Exp, scale=m["rD"][:, 0, i:i + 1]), "e2")
                bank_free[bk] = (t,)
            yield
            wait("dve", t)
            t = emit("dve", lambda e: e.scalar_tensor_tensor(
                tA, tB, 1.0, tA, ALU.min, ALU.add), "g2")
            wait("dve", t)
            t = emit("dve", lambda e: e.scalar_tensor_tensor(
                x[:, :, :], tA, -1.0, x[:, :, :], ALU.add, ALU.add), "x2")
            tab_free[s] = (t,)
            wait("dve", t)
            yield

            t_h = yield from layer_norm(s)
            t_S = column_sums(s, W3, t_h)
            yield
            wait("pe", *t_w["L3"])
            banks = yield from gat256(s, hT[s], W3, t_h, 0.01, maskT["ne"])
            for i, (bk, t) in enumerate(banks):
                t = row_sum_inverse(s, bk, i, t)
                wait("act", t, *tab_free[s])
                t = emit("act", lambda e, i=i, bk=bk: e.activation(
                    tA[:, i, :], bank[bk][:, 0:256], ACT.Copy, scale=m["rD"][:, 0, i:i + 1]), "y3")
                bank_free[bk] = (t,)
            yield
            wait("dve", t, t_S)
            for i in range(NBLK):
                t = emit("dve", lambda e, i=i: e.scalar_tensor_tensor(
                    tA[:, i, :], m["Sb"][:, :], empty["ne"][:, i:i + 1], tA[:, i, :], ALU.mult, ALU.add), "y32")
            wait("dve", t)
            t = emit("dve", lambda e: e.scalar_tensor_tensor(
                x[:, :, :], tA, 0.0, x[:, :, :], ALU.max, ALU.add), "x3")
            tab_free[s] = (t,)
            wait("sp", t)
            t_store[s] = emit("sp", lambda e: e.dma_start(o_v[b], x[:, :, :]), f"out{s}", 16)
            if b + STREAMS < B:
                wait("sp", t_store[s])
                t_x[s] = emit("sp", lambda e: e.dma_start(x[:, :, :], x_v[b + STREAMS]), f"x{s}", 16)
            yield

        live = []
        nxt = [s for s in range(STREAMS)]

        def chain(s, lead):
            for _ in range(lead):
                yield
            for b in range(s, B, STREAMS):
                yield from batch(b)

        live = [chain(s, LEAD * s) for s in range(STREAMS)]
        while live:
            for g in list(live):
                try:
                    next(g)
                except StopIteration:
                    live.remove(g)
        for s in range(STREAMS):
            wait("sp", t_store[s])

        block = ctx.enter_context(nc.Block())

        @block.sync
        def _(e):
            L.play("sp", e)

        @block.tensor
        def _(e):
            L.play("pe", e)

        @block.vector
        def _(e):
            L.play("dve", e)

        @block.scalar
        def _(e):
            L.play("act", e)

        @block.gpsimd
        def _(e):
            L.play("pool", e)


LEAD = 20

_INS = ["x", "adj", "L0_gnn_W", "L0_gnn_a", "L1_gnn_mlp1_w", "L1_gnn_mlp1_b", "L1_gnn_mlp2_w", "L1_gnn_mlp2_b",
        "L1_gnn_W_fc", "L1_gnn_a_fc", "L1_gnn_W_hand", "L1_gnn_a_hand", "L2_gnn_W", "L2_gnn_a", "L3_gnn_W",
        "L3_gnn_a"]


def kernel(**inputs):
    import numpy as _np
    import concourse.bacc as _bacc
    from concourse import mybir as _mybir
    from concourse.bass_utils import run_bass_kernel_spmd as _run

    nc = _bacc.Bacc("TRN2", target_bir_lowering=False, num_devices=1)
    arrays, args = {}, []
    for name in _INS:
        a = _np.ascontiguousarray(inputs[name])
        arrays[f"in_{name}_dram"] = a
        args.append(nc.dram_tensor(f"in_{name}_dram", a.shape, _mybir.dt.from_np(a.dtype), kind="ExternalInput").ap())
    args.append(nc.dram_tensor("out_0_dram", (B, N, F), F32, kind="ExternalOutput").ap())
    build(nc, *args)
    r = _run(nc, [arrays], core_ids=[0])
    return r.results[0]["out_0_dram"]
```

```python
from contextlib import ExitStack

import concourse.bass as bass
from concourse import mybir

ALU = mybir.AluOpType
ACT = mybir.ActivationFunctionType
F32 = mybir.dt.float32
F32R = mybir.dt.float32r
I32 = mybir.dt.int32
U8 = mybir.dt.uint8
AXX = mybir.AxisListType.X

B, N, F = 32, 512, 256
NBLK = 4
TINY = 1e-37
EPS = 1e-5
SHIFT = 30.0
LANES = 3
LANE_BANKS = {0: (0, 1, 2), 1: (3, 4, 5), 2: (6, 7), 3: tuple(range(8))}
XSLOTS = 4


class Queues:

    PARTS = ("pe", "dve", "act", "pool", "sp")

    def __init__(self, nc, ctx):
        self.nc, self.ctx = nc, ctx
        self.q, self.sems, self.count = {}, {}, {}
        self.lane = "I"
        self.pending = {}
        self.rank = 0

    def emit(self, part, fn, sig=None, ns=60, by=1):
        waits = self.pending.pop((self.lane, part), [])
        token = None
        if sig is not None:
            name = f"{part}_{self.lane}_{STAGE_OF.get(sig, sig)}"
            if name not in self.sems:
                self.sems[name] = self.ctx.enter_context(self.nc.semaphore(name))
                self.count[name] = 0
            self.count[name] += by
            token = (name, self.count[name])
        self.q.setdefault((self.lane, part), []).append((fn, waits, token, by, ns, self.rank))
        return token

    def wait(self, part, *tokens):
        self.pending.setdefault((self.lane, part), []).extend(tokens)

    def merge(self):
        assert not any(self.pending.values())
        at = {k: 0 for k in self.q}
        free = dict.fromkeys(self.PARTS, 0.0)
        done = {}
        ready = {}
        order = {p: [] for p in self.PARTS}
        left = sum(len(v) for v in self.q.values())
        while left:
            best = None
            for (lane, part), n in at.items():
                queue = self.q[(lane, part)]
                if n == len(queue):
                    continue
                key = (lane, part, n)
                if key not in ready:
                    waits = queue[n][1]
                    if not all(w in done for w in waits):
                        continue
                    ready[key] = max([done[w] for w in waits], default=0.0)
                start = max(free[part], ready[key])
                rank = (start, queue[n][5])
                if best is None or rank < best[0]:
                    best = (rank, lane, part)
            assert best is not None, "the lanes wait for each other"
            (start, _), lane, part = best
            item = self.q[(lane, part)][at[(lane, part)]]
            at[(lane, part)] += 1
            left -= 1
            free[part] = start + (50 if part == "sp" else item[4])
            if item[2] is not None:
                done[item[2]] = start + item[4] + LAT[part]
            order[part].append(item)
        return order

    def play(self, part, order, eng):
        seen = {}
        for fn, waits, token, by, _, _ in order[part]:
            for name, value in waits:
                if seen.get(name, 0) < value:
                    seen[name] = value
                    eng.wait_ge(self.sems[name], value)
            ins = fn(eng)
            if token is not None:
                ins.then_inc(self.sems[token[0]], by)
        for name, value in self.pending.pop(("end", part), []):
            eng.wait_ge(self.sems[name], value)


STAGE_OF = {sig: stage for stage, sigs in {
    "norm": ("st", "mv", "ve", "rs", "hn", "hT", "hThi", "hTlo"),
    "score": ("sc", "tm", "TM", "T", "u", "u1", "u2", "E"),
    "sums": ("hs", "S", "Sb"),
    "P": ("row", "P", "Phi", "Plo"),
    "hw": ("h", "raw", "hwf", "hwhi", "hwlo", "hwhi0", "hwlo0", "wch", "wcl"),
    "mlp": ("m1", "m2", "o1hi", "o1lo", "o3hi", "o3lo"),
    "att": ("att", "att0", "attf", "Df", "D", "rD", "rrow"),
    "post": ("yT", "yTT", "y0", "e0", "x0", "m0", "x0b", "yf", "ef", "mf", "ef2", "gf", "resf", "o2", "o2hi", "o2lo",
             "yh", "yh2", "eh", "mh", "eh2", "gh", "gh2", "xh", "r3", "e2", "g2", "x2", "y3", "y32", "x3"),
    "load": ("whi", "wlo", "wT", "wTe", "wA", "wAh", "wAl", "az"),
    "mask": ("mrow", "emp", "mT", "mTe", "emp2", "self", "mask"),
}.items() for sig in sigs}

LAT = {"pe": 180, "dve": 80, "act": 120, "pool": 100, "sp": 1500}


def build(nc, x_d, adj_d, L0_W, L0_a, m1_w, m1_b, m2_w, m2_b, fc_w, fc_a, ha_w, ha_a, L2_W, L2_a, L3_W, L3_a, out_d):
    ctx = ExitStack()
    with ctx:
        def sb(name, shape, dt=F32):
            return ctx.enter_context(nc.sbuf_tensor(name, shape, dt))

        L = Queues(nc, ctx)
        emit, wait = L.emit, L.wait

        bank = [ctx.enter_context(nc.psum_tensor(f"bank{i}", [128, 512], F32)) for i in range(8)]
        bank_free = [() for _ in range(8)]
        turn = {0: 0, 1: 0, 2: 0, 3: 0}

        identr = sb("identr", [128, 128], F32R)
        ident = identr[:, :].bitcast(F32)
        kshift = sb("kshift", [128, 1])
        minus1 = sb("minus1", [128, 1])
        mhalf = sb("mhalf", [128, NBLK])
        maskT = {k: sb(f"mask_{k}", [128, NBLK, N], U8) for k in ("ne", "gt", "self")}
        empty = {k: sb(f"empty_{k}", [128, NBLK]) for k in ("ne", "gt")}
        b1 = sb("b1", [128, 4])
        b2 = sb("b2", [128, 2])

        def weights(name, kb, fo, nq):
            return {"hi": sb(name + "_hi", [128, kb, fo + nq], F32R),
                    "lo": sb(name + "_lo", [128, kb, fo + nq], F32R), "kb": kb, "fo": fo, "nq": nq}

        W0 = weights("w0", 2, 256, 8)
        WM1 = weights("wm1", 2, 512, 0)
        WFC = weights("wfc", 4, 512, 2)
        WM2 = weights("wm2", 4, 256, 0)
        WHA = weights("wha", 2, 256, 2)
        W2 = weights("w2", 2, 256, 2)
        W3 = weights("w3", 2, 256, 2)

        PARTS2 = ("hi", "lo")
        xs = [sb(f"x{i}", [128, NBLK, F]) for i in range(XSLOTS)]
        raw = [sb(f"raw{s}", [128, NBLK, 264]) for s in range(LANES)]
        X = [[raw[s][:, :, :].rearrange("p b n -> p (b n)")[:, 0:1024].rearrange("p (a n) -> p a n", a=2),
              sb(f"X{s}", [128, 2, 512])[:, :, :]] for s in range(LANES)]
        P = [{p: sb(f"P{s}{p}", [128, NBLK, N], F32R) for p in PARTS2} for s in range(LANES)]
        hT = [{p: P[s][p][:, 0:2, :] for p in PARTS2} for s in range(LANES)]
        oT = {p: sb(f"oT{p}", [128, 4, N], F32R) for p in PARTS2}
        rT = {p: sb(f"rT{p}", [128, 2, N], F32R) for p in PARTS2}
        hws = [{p: sb(f"hw{s}{p}", [128, NBLK, 264], F32R) for p in PARTS2} for s in range(LANES)]
        wdf = [{p: sb(f"wdf{s}{p}", [128, NBLK], F32R) for p in PARTS2} for s in range(LANES)]
        rowt = [sb(f"rowt{s}", [128, N]) for s in range(LANES)]
        NH = 4
        sm = [{
            "st": sb(f"st{s}", [128, NBLK, 6]), "mv": sb(f"mv{s}", [128, NBLK, 2]),
            "ve": sb(f"ve{s}", [128, NBLK]), "rs": sb(f"rs{s}", [128, NBLK]),
            "tm": sb(f"tm{s}", [128, NH]),
            "T": sb(f"T{s}", [128, NH]), "A": sb(f"A{s}", [128, 3, NH, NBLK]),
            "E": sb(f"E{s}", [128, 3, NH, NBLK]),
            "D": sb(f"D{s}", [128, NH, NBLK]), "rD": sb(f"rD{s}", [128, NH, NBLK]),
            "hs": sb(f"hs{s}", [128, 2]), "hsr": sb(f"hsr{s}", [128, 2, 2], F32R),
            "Sb": sb(f"Sb{s}", [128, F]),
        } for s in range(LANES)]

        P_free = [[()] * NBLK for _ in range(LANES)]
        raw_free = [()] * LANES
        st_free_of = [[(), ()] for _ in range(LANES)]
        hw_free = [()] * LANES
        rowt_free = [()] * LANES
        oT_free = ()
        rT_free = ()
        x_free = [()] * XSLOTS

        def take_bank(s):
            ring = LANE_BANKS[s]
            i = ring[turn[s] % len(ring)]
            turn[s] += 1
            assert bank_free[i] is not None
            wait("pe", *bank_free[i])
            bank_free[i] = None
            return i

        def f32(ap):
            return ap.bitcast(F32)

        def d_ns(n, psum=False):
            return (130 if psum else 65) + 1.04 * n

        def a_ns(n, ptr=0):
            return 190 + 60 * ptr + 0.83 * n

        def p_ns(n):
            return 60 + 2.2 * n

        TR_NS = 107

        L.lane, L.rank = "I", -1
        id_st = X[2][1][:, 0, 0:128]
        t0 = emit("pool", lambda e: e.memset(id_st, 0.0), "c0")
        wait("pool", t0)
        t0 = emit("pool", lambda e: e.affine_select(out=id_st, in_=id_st, compare_op=ALU.not_equal,
                                                      fill=1.0, base=0, pattern=[[-1, 128]],
                                                      channel_multiplier=1), "id")
        emit("pool", lambda e: e.memset(kshift[:, :], SHIFT))
        emit("pool", lambda e: e.memset(minus1[:, :], -1.0))
        t_const = emit("pool", lambda e: e.memset(mhalf[:, :], -0.5), "const")
        wait("dve", t0)
        t_id = emit("dve", lambda e: e.tensor_copy(identr[:, :], id_st), "idr")

        x_v = x_d.rearrange("n (p b) f -> n p b f", b=NBLK)
        o_v = out_d.rearrange("n (p b) f -> n p b f", b=NBLK)
        t_x = {}

        def load_x(b):
            wait("sp", *x_free[b % XSLOTS])
            t_x[b] = emit("sp", lambda e: e.dma_start(xs[b % XSLOTS][:, :, :], x_v[b]), f"xin{b % XSLOTS}",
                          ns=3000, by=16)

        load_x(0)

        wT = X[1][0]
        a_st = X[1][1][:, 0, 0:32].rearrange("p (k q) -> p k q", q=8)
        st_free = [[], [t_id]]
        misc = {"wT": (), "a": ()}

        def load_weights(w, w_d, a_fill):
            kb, fo, nq = w["kb"], w["fo"], w["nq"]
            wv = w_d.rearrange("(k p) n -> p k n", p=128)
            per = 1024 // fo
            tiles, toks, n_c = [], [], (kb + per - 1) // per
            for c in range(n_c):
                k0, k1 = c * per, min(kb, (c + 1) * per)
                dst = X[2][c].rearrange("p a n -> p (a n)")[:, 0:(k1 - k0) * fo].rearrange(
                    "p (k n) -> p k n", n=fo)
                wait("sp", *st_free[c])
                toks.append(emit("sp", lambda e, dst=dst, k0=k0, k1=k1: e.dma_start(dst, wv[:, k0:k1, :]),
                                 f"wl{c}", ns=3500, by=16))
                tiles += [dst[:, k, :] for k in range(k1 - k0)]
            ta_ = None
            if nq:
                wait("dve", *misc["a"])
                tz = emit("dve", lambda e: e.memset(a_st, 0.0), "az")
                wait("sp", tz)
                ta_ = a_fill()
            wait("act", *toks)
            for k in range(kb):
                th = emit("act", lambda e, k=k: e.copy(w["hi"][:, k, 0:fo], tiles[k]), "whi", ns=a_ns(fo))
            wait("dve", *toks, th)
            for k in range(kb):
                tl = emit("dve", lambda e, k=k: e.tensor_tensor(w["lo"][:, k, 0:fo], tiles[k], f32(w["hi"][:, k, 0:fo]),
                                                                ALU.subtract), "wlo", ns=d_ns(fo))
            free = [tl]
            if nq:
                ob = fo // 128
                wait("pe", *toks, ta_, t_id)
                for k in range(kb):
                    bk = take_bank(3)
                    for o in range(ob):
                        tw = emit("pe", lambda e, k=k, o=o, bk=bk: e.transpose(
                            bank[bk][:, o * 128:(o + 1) * 128], tiles[k][:, o * 128:(o + 1) * 128],
                            ident[:, :]), "wT", ns=TR_NS)
                    wait("dve", tw, *misc["wT"])
                    te = emit("dve", lambda e, bk=bk, ob=ob: e.tensor_copy(
                        wT[:, 0, 0:ob * 128], bank[bk][:, 0:ob * 128]), "wTe", ns=d_ns(ob * 128))
                    bank_free[bk] = (te,)
                    wait("pe", te)
                    bk = take_bank(3)
                    for o in range(ob):
                        tp = emit("pe", lambda e, o=o, bk=bk, ob=ob: e.matmul(
                            bank[bk][:, 0:nq], wT[:, 0, o * 128:(o + 1) * 128], a_st[:, o, 0:nq],
                            start=(o == 0), stop=(o == ob - 1)), "wA")
                    misc["wT"] = misc["a"] = (tp,)
                    wait("dve", tp)
                    te = emit("dve", lambda e, k=k, bk=bk: e.tensor_copy(w["hi"][:, k, fo:fo + nq], bank[bk][:, 0:nq]),
                              "wAh")
                    wait("dve", te)
                    te = emit("dve", lambda e, k=k, bk=bk: e.tensor_tensor(
                        w["lo"][:, k, fo:fo + nq], bank[bk][:, 0:nq], f32(w["hi"][:, k, fo:fo + nq]),
                        ALU.subtract), "wAl")
                    bank_free[bk] = (te,)
                free.append(tw)
            for c in range(n_c):
                st_free[c] = free
            return [tl] + ([te] if nq else [])

        def a_dma(dst, src):
            return emit("sp", lambda e: e.dma_start(dst, src, allow_slow_non_contiguous=True), "al", ns=2500, by=16)

        def fill_heads():
            for h in range(4):
                for t in range(2):
                    p0 = (h % 2) * 64
                    tok = a_dma(a_st[p0:p0 + 64, h // 2, t * 4 + h:t * 4 + h + 1],
                                L0_a[h, t * 64:(t + 1) * 64].rearrange("(p o) -> p o", o=1))
            return tok

        def fill_col(a_d, ob):
            def go():
                for t in range(2):
                    tok = a_dma(a_st[:, 0:ob, t],
                                a_d[t * ob * 128:(t + 1) * ob * 128, 0].rearrange("(k p) -> p k", p=128))
                return tok
            return go

        t_w = {}
        t_w["L0"] = load_weights(W0, L0_W, fill_heads)

        adj_v = adj_d.rearrange("(p b) j -> p b j", b=NBLK)
        wait("dve", *misc["wT"], *misc["a"])
        t_pe, t_red = (), ()
        for half in range(2):
            wait("sp", *st_free[half])
            src = X[2][half].bitcast(I32)
            t_adj = emit("sp", lambda e, src=src, half=half: e.dma_start(
                src, adj_v[:, 2 * half:2 * half + 2, :]), f"wl{half}", ns=3500, by=16)
            mrow = {"ne": X[1][0], "gt": X[1][1]}
            wait("dve", t_adj, *t_pe, *t_red)
            for k, op in (("ne", ALU.not_equal), ("gt", ALU.is_gt)):
                t_m = emit("dve", lambda e, k=k, op=op, src=src, mrow=mrow: e.tensor_scalar(
                    mrow[k][:, :, :], src, 0.0, None, op), "mrow", ns=d_ns(1024))
            st_free[half] = [t_m]
            wait("dve", t_m)
            for k in ("ne", "gt"):
                t_r = emit("dve", lambda e, k=k, half=half, mrow=mrow: e.tensor_reduce(
                    empty[k][:, 2 * half:2 * half + 2], mrow[k][:, :, :], AXX, ALU.max), "emp", ns=d_ns(1024))
            t_red = (t_r,)
            wait("pe", t_m, t_id)
            for k in ("ne", "gt"):
                for bj in range(NBLK):
                    bk = take_bank(3)
                    for b in range(2):
                        tp = emit("pe", lambda e, k=k, b=b, bj=bj, bk=bk, mrow=mrow: e.transpose(
                            bank[bk][:, b * 128:(b + 1) * 128], mrow[k][:, b, bj:N:NBLK], ident[:, :]), "mT",
                            ns=TR_NS)
                    wait("dve", tp)
                    t_ev = emit("dve", lambda e, k=k, bj=bj, bk=bk, half=half: e.tensor_copy(
                        maskT[k][:, bj, half * 256:(half + 1) * 256], bank[bk][:, 0:256]), "mTe", ns=d_ns(256))
                    bank_free[bk] = (t_ev,)
            t_pe = (tp,)
        misc["wT"] = misc["a"] = (tp, t_r)
        wait("dve", t_r)
        for k in ("ne", "gt"):
            t_emp = emit("dve", lambda e, k=k: e.tensor_scalar(empty[k][:, :], empty[k][:, :], -1.0, 1.0,
                                                               ALU.mult, ALU.add), "emp2")
        wait("dve", t_ev)
        t_cp = emit("dve", lambda e: e.tensor_copy(maskT["self"][:, :, :], maskT["gt"][:, :, :]), "self",
                    ns=d_ns(2048))
        wait("dve", t_cp)
        for bj in range(NBLK):
            t_mask = emit("dve", lambda e, bj=bj: e.tensor_tensor(
                maskT["self"][:, bj, bj * 128:(bj + 1) * 128], maskT["self"][:, bj, bj * 128:(bj + 1) * 128],
                ident[:, :], ALU.max), "mask", ns=d_ns(128))

        t_bias = emit("sp", lambda e: e.dma_start(b1[:, :], m1_b.rearrange("(k p) -> p k", p=128),
                                                  allow_slow_non_contiguous=True), "b", ns=2500, by=16)
        t_bias = emit("sp", lambda e: e.dma_start(b2[:, :], m2_b.rearrange("(k p) -> p k", p=128),
                                                  allow_slow_non_contiguous=True), "b", ns=2500, by=16)
        t_w["m1"] = load_weights(WM1, m1_w, None)
        t_w["fc"] = load_weights(WFC, fc_w, fill_col(fc_a, 4))
        t_w["m2"] = load_weights(WM2, m2_w, None)
        t_w["ha"] = load_weights(WHA, ha_w, fill_col(ha_a, 2))
        t_w["L2"] = load_weights(W2, L2_W, fill_col(L2_a, 2))
        t_w["L3"] = load_weights(W3, L3_W, fill_col(L3_a, 2))
        ended = tuple(st_free[0]) + tuple(st_free[1]) + misc["wT"]
        for s_ in (1, 2):
            raw_free[s_] = ended
            st_free_of[s_] = [ended, ended]

        def mm3(out, a, b, first, last, sig=None, group=True, n=512):
            t = None
            for q, (u, v) in enumerate(((a[0], b[0]), (a[0], b[1]), (a[1], b[0]))):
                st, sp = first and q == 0, last and q == 2
                t = emit("pe", lambda e, u=u, v=v, st=st, sp=sp: e.matmul(
                    out, u, v, start=st, stop=sp, skip_group_check=not group),
                    sig if (sp and sig) else None, ns=max(107, n / 2.4)) or t
            return t

        def layer_norm(s, x, t_in):
            m = sm[s]
            hn = X[s][0].rearrange("p a (b n) -> p (a b) n", n=256)
            wait("dve", *t_in)
            for b in range(NBLK):
                t = emit("dve", lambda e, b=b: e.bn_stats(m["st"][:, b, :], x[:, b, :]), "st", ns=335)
            wait("dve", t)
            for b in range(NBLK):
                t = emit("dve", lambda e, b=b: e.bn_aggr(m["mv"][:, b, :], m["st"][:, b, :]), "mv", ns=75)
            wait("dve", t)
            t = emit("dve", lambda e: e.tensor_scalar(m["ve"][:, :], m["mv"][:, :, 1], EPS, None, ALU.add), "ve")
            wait("pool", t, t_const)
            t = emit("pool", lambda e: e.tensor_tensor(m["rs"][:, :], m["ve"][:, :], mhalf[:, :], ALU.pow), "rs",
                     ns=960)
            wait("dve", t, *raw_free[s])
            for b in range(NBLK):
                t = emit("dve", lambda e, b=b: e.tensor_scalar(
                    hn[:, b, :], x[:, b, :], m["mv"][:, b, 0:1], m["rs"][:, b:b + 1],
                    ALU.subtract, ALU.mult), "hn", ns=323)
            wait("pe", t, t_id)
            for k in range(2):
                bk = take_bank(s)
                for b in range(NBLK):
                    t = emit("pe", lambda e, b=b, k=k, bk=bk: e.transpose(
                        bank[bk][:, b * 128:(b + 1) * 128], hn[:, b, k * 128:(k + 1) * 128], ident[:, :]), "hT",
                        ns=TR_NS)
                raw_free[s] = (t,)
                wait("act", t, *P_free[s][0])
                t = emit("act", lambda e, k=k, bk=bk: e.activation(
                    hT[s]["hi"][:, k, :], bank[bk][:, :], ACT.Relu, accum_out=m["hs"][:, k:k + 1]), "hThi",
                    ns=a_ns(550))
                wait("dve", t, *P_free[s][0])
                t = emit("dve", lambda e, k=k, bk=bk: e.scalar_tensor_tensor(
                    hT[s]["lo"][:, k, :], bank[bk][:, :], 0.0, f32(hT[s]["hi"][:, k, :]),
                    ALU.max, ALU.subtract), "hTlo", ns=602)
                bank_free[bk] = (t,)
            return t

        def scores(s, t_raw, alpha, nh):
            m = sm[s]
            sc = raw[s][:, :, 256:256 + 2 * nh].rearrange("p b q -> p q b")
            wait("dve", t_raw)
            t = emit("dve", lambda e: e.tensor_reduce(m["tm"][:, 0:nh], sc[:, nh:2 * nh, :], AXX, ALU.max),
                     "tm", ns=80)
            wait("pe", t)
            bm = take_bank(s)
            for h in range(nh):
                t = emit("pe", lambda e, h=h: e.transpose(
                    bank[bm][:, h * 128:(h + 1) * 128], m["tm"][:, h:h + 1].broadcast_to([128, 128]),
                    ident[:, :]), "TM", ns=TR_NS)
            wait("dve", t)
            v2 = bank[bm][:, 0:nh * 128].rearrange("p (h n) -> p h n", h=nh)
            t = emit("dve", lambda e: e.tensor_reduce(m["T"][:, 0:nh], v2, AXX, ALU.max), "T",
                     ns=d_ns(128 * nh, True))
            bank_free[bm] = (t,)
            wait("dve", t)
            Tb = m["T"][:, 0:nh].rearrange("p (h o) -> p h o", o=1).broadcast_to([128, nh, NBLK])
            emit("dve", lambda e: e.tensor_tensor(m["A"][:, 0, 0:nh, :], sc[:, nh:2 * nh, :], Tb,
                                                  ALU.subtract))
            t = emit("dve", lambda e: e.tensor_tensor(m["A"][:, 2, 0:nh, :], sc[:, 0:nh, :], Tb, ALU.add),
                     "u")
            wait("dve", t)
            t = emit("dve", lambda e: e.tensor_scalar(m["A"][:, 1, 0:nh, :], m["A"][:, 0, 0:nh, :],
                                                      1.0 - alpha, None, ALU.mult), "u1")
            emit("dve", lambda e: e.tensor_scalar(m["A"][:, 2, 0:nh, :], m["A"][:, 2, 0:nh, :],
                                                  -(1.0 - alpha), 0.0, ALU.mult, ALU.min))
            wait("dve", t)
            t = emit("dve", lambda e: e.tensor_scalar(m["A"][:, 0, 0:nh, :], m["A"][:, 0, 0:nh, :],
                                                      alpha, None, ALU.mult), "u2")
            wait("act", t, t_const)
            return emit("act", lambda e: e.activation(m["E"][:, :, 0:nh, :], m["A"][:, :, 0:nh, :], ACT.Exp,
                                                      bias=kshift[:, 0:1]), "E", ns=300)

        def row_of(s, src, t_src):
            wait("pe", t_src)
            bk = take_bank(s)
            for b in range(NBLK):
                t = emit("pe", lambda e, b=b: e.transpose(
                    bank[bk][:, b * 128:(b + 1) * 128], src[:, b:b + 1].broadcast_to([128, 128]),
                    ident[:, :]), "row", ns=TR_NS)
            return bk, t

        def build_P(s, h, mask, t_E, row):
            m = sm[s]
            bk, t_row = row
            out = []
            for j in range(NBLK):
                st = X[s][1][:, j % 2, :]
                wait("dve", t_row, t_E, *st_free_of[s][j % 2])
                r = m["E"][:, 1, h, j:j + 1]
                if mask is None:
                    t = emit("dve", lambda e, r=r, st=st: e.tensor_scalar(
                        st, bank[bk][:, :], r, None, ALU.max), "P", ns=662)
                else:
                    t = emit("dve", lambda e, j=j, r=r, st=st: e.scalar_tensor_tensor(
                        st, bank[bk][:, :], r, mask[:, j, :], ALU.max, ALU.mult), "P", ns=662)
                wait("act", t, *P_free[s][j])
                th = emit("act", lambda e, st=st, j=j: e.copy(P[s]["hi"][:, j, :], st), "Phi", ns=520)
                wait("pool", th, *P_free[s][j])
                tl = emit("pool", lambda e, st=st, j=j: e.tensor_tensor(
                    P[s]["lo"][:, j, :], st, f32(P[s]["hi"][:, j, :]), ALU.subtract), "Plo", ns=1225)
                st_free_of[s][j % 2] = (tl,)
                out.append(tl)
            bank_free[bk] = (t,)
            return out

        def project_raw(s, src, w, t_src, f0):
            n = 256 + w["nq"]
            wait("pe", *t_src)
            for b in range(NBLK):
                bk = take_bank(s)
                cols = slice(b * 128, (b + 1) * 128)
                for k in range(w["kb"]):
                    tp = mm3(bank[bk][:, 0:n], (src["hi"][:, k, cols], src["lo"][:, k, cols]),
                             (w["hi"][:, k, f0:f0 + n], w["lo"][:, k, f0:f0 + n]), k == 0, k == w["kb"] - 1, "h",
                             n=n)
                wait("act", tp, *raw_free[s])
                t = emit("act", lambda e, b=b, bk=bk: e.copy(raw[s][:, b, 0:n], bank[bk][:, 0:n]), "raw",
                         ns=a_ns(n))
                bank_free[bk] = (t,)
            return t, tp

        def scale_split(s, t_E, hw, free):
            m = sm[s]
            for b in range(NBLK):
                wj = m["E"][:, 0, 0, b:b + 1]
                wait("act", t_E, *free)
                t = emit("act", lambda e, b=b, wj=wj: e.activation(
                    hw["hi"][:, b, 0:256], raw[s][:, b, 0:256], ACT.Copy, scale=wj), "hwhi", ns=411)
                wait("dve", t, *free)
                t = emit("dve", lambda e, b=b, wj=wj: e.scalar_tensor_tensor(
                    hw["lo"][:, b, 0:256], raw[s][:, b, 0:256], wj, f32(hw["hi"][:, b, 0:256]),
                    ALU.mult, ALU.subtract), "hwlo", ns=340)
            raw_free[s] = (t,)
            return t

        def project_scaled(s, src, w, t_E, hw, free, fs):
            m, kb = sm[s], w["kb"]
            for b in range(NBLK):
                bk = take_bank(s)
                cols = slice(b * 128, (b + 1) * 128)
                for k in range(kb):
                    tp = mm3(bank[bk][:, 0:256], (src["hi"][:, k, cols], src["lo"][:, k, cols]),
                             (w["hi"][:, k, fs], w["lo"][:, k, fs]), k == 0, k == kb - 1, "h", n=256)
                wj = m["E"][:, 0, 0, b:b + 1]
                wait("act", tp, t_E, *free)
                t = emit("act", lambda e, b=b, bk=bk, wj=wj: e.activation(
                    hw["hi"][:, b, 0:256], bank[bk][:, 0:256], ACT.Copy, scale=wj), "hwhi", ns=411)
                wait("dve", t, t_E, *free)
                t = emit("dve", lambda e, b=b, bk=bk, wj=wj: e.scalar_tensor_tensor(
                    hw["lo"][:, b, 0:256], bank[bk][:, 0:256], wj, f32(hw["hi"][:, b, 0:256]),
                    ALU.mult, ALU.subtract), "hwlo", ns=463)
                bank_free[bk] = (t,)
            return t, tp

        def weight_columns(src, hi, lo, t_E, free):
            wait("dve", t_E, *free)
            t = emit("dve", lambda e: e.tensor_copy(hi, src), "wch")
            wait("dve", t)
            return emit("dve", lambda e: e.tensor_tensor(lo, src, f32(hi), ALU.subtract), "wcl")

        def column_sums(s, w, t_hs):
            m = sm[s]
            wait("dve", t_hs)
            t = emit("dve", lambda e: e.tensor_copy(m["hsr"][:, :, 0], m["hs"][:, :]), "hs")
            wait("dve", t)
            t = emit("dve", lambda e: e.tensor_tensor(m["hsr"][:, :, 1], m["hs"][:, :], f32(m["hsr"][:, :, 0]),
                                                      ALU.subtract), "hs")
            wait("pe", t)
            bk = take_bank(s)
            for k in range(2):
                a = tuple(m["hsr"][:, k, p:p + 1].broadcast_to([128, 128]) for p in range(2))
                t = mm3(bank[bk][:, 0:256], a, (w["hi"][:, k, 0:256], w["lo"][:, k, 0:256]), k == 0, k == 1, "S", n=256)
            wait("act", t)
            t = emit("act", lambda e: e.activation(m["Sb"][:, :], bank[bk][:, 0:256], ACT.Copy, scale=1.0 / N),
                     "Sb", ns=a_ns(256))
            bank_free[bk] = (t,)
            return t

        def gat256(s, src, w, t_src, alpha, mask, evacuate):
            m = sm[s]
            t_raw, t_read = project_raw(s, src, w, t_src, 0)
            if src is hT[s]:
                P_free[s] = [(t_read,)] * NBLK
            t_E = scores(s, t_raw, alpha, 1)
            row = row_of(s, m["E"][:, 2, 0, :], t_E)
            t_P = build_P(s, 0, mask, t_E, row)
            hw, free = hws[s], hw_free[s]
            wc = m["E"][:, 0, 0, :].rearrange("p (b o) -> p b o", o=1).broadcast_to([128, NBLK, 2])
            t_c = weight_columns(wc, hw["hi"][:, :, 256:258], hw["lo"][:, :, 256:258], t_E, free)
            t_h = scale_split(s, t_E, hw, free)
            wait("pe", t_h, t_c)
            for i in range(NBLK):
                bk = take_bank(s)
                cols = slice(i * 128, (i + 1) * 128)
                for j in range(NBLK):
                    wait("pe", t_P[j])
                    t = mm3(bank[bk][:, 0:258], (P[s]["hi"][:, j, cols], P[s]["lo"][:, j, cols]),
                            (hw["hi"][:, j, 0:258], hw["lo"][:, j, 0:258]), j == 0, j == NBLK - 1, "att", n=258)
                wait("dve", t)
                td = emit("dve", lambda e, bk=bk, i=i: e.tensor_scalar(
                    m["D"][:, 0, i:i + 1], bank[bk][:, 256:257], TINY, None, ALU.max), "D", ns=130)
                wait("dve", td)
                td = emit("dve", lambda e, i=i: e.reciprocal(m["rD"][:, 0, i:i + 1], m["D"][:, 0, i:i + 1]), "rD",
                          ns=70)
                bank_free[bk] = evacuate(i, bk, td)
            P_free[s] = [(t,)] * NBLK
            hw_free[s] = (t,)

        def blocks(tile):
            return tile.rearrange("p a (b n) -> p (a b) n", n=256)

        t_layer = {}

        def layer0(b):
            s, x = b % LANES, xs[b % XSLOTS]
            m = sm[s]
            t_h = layer_norm(s, x, (t_x[b],))
            t_raw, t_read = project_raw(s, hT[s], W0, (t_h, *t_w["L0"]), 0)
            P_free[s] = [(t_read,)] * NBLK
            t_E = scores(s, t_raw, 0.2, 4)
            hw, free = hws[s], hw_free[s]
            hv = {p: hw[p][:, :, :].rearrange("p b (h n) -> p b h n", n=66) for p in PARTS2}
            row = row_of(s, m["E"][:, 2, 0, :], t_E)
            rv = raw[s][:, :, 0:256].rearrange("p b (h n) -> p b h n", n=64)
            wait("dve", t_E)
            for bl in range(NBLK):
                wb = m["E"][:, 0, :, bl:bl + 1].broadcast_to([128, 4, 64])
                t = emit("dve", lambda e, bl=bl, wb=wb: e.tensor_tensor(rv[:, bl], rv[:, bl], wb, ALU.mult), "hwf",
                         ns=d_ns(256))
            for bp in range(2):
                bs = slice(2 * bp, 2 * bp + 2)
                wait("act", t, *free)
                for bl in (2 * bp, 2 * bp + 1):
                    t1 = emit("act", lambda e, bl=bl: e.copy(hv["hi"][:, bl, :, 0:64], rv[:, bl]), "hwhi0", ns=307)
                wait("pool", t1, *free)
                for bl in (2 * bp, 2 * bp + 1):
                    t_hw = emit("pool", lambda e, bl=bl: e.tensor_tensor(
                        hv["lo"][:, bl, :, 0:64], rv[:, bl], f32(hv["hi"][:, bl, :, 0:64]), ALU.subtract),
                        "hwlo0", ns=687)
            raw_free[s] = (t_hw,)
            wait("dve", t_mask)
            t_P = build_P(s, 0, maskT["ne"], t_E, row)
            for bl in range(NBLK):
                wc = m["E"][:, 0, :, bl:bl + 1].broadcast_to([128, 4, 2])
                t_c = weight_columns(wc, hv["hi"][:, bl, :, 64:66], hv["lo"][:, bl, :, 64:66], t_E, free)
            wait("pe", t_hw, t_c)
            y_free = raw_free[s]
            for h in range(4):
                if h < 3:
                    row = row_of(s, m["E"][:, 2, h + 1, :], t_E)
                bk = take_bank(s)
                for j in range(NBLK):
                    wait("pe", t_P[j])
                    t = mm3(bank[bk][0:66, :], (hv["hi"][:, j, h, :], hv["lo"][:, j, h, :]),
                            (P[s]["hi"][:, j, :], P[s]["lo"][:, j, :]), j == 0, j == NBLK - 1, "att0")
                P_free[s] = [(t,)] * NBLK
                t_att = t
                if h < 3:
                    t_P = build_P(s, h + 1, maskT["ne"], t_E, row)
                wait("act", t_att, *rowt_free[s])
                t = emit("act", lambda e, bk=bk: e.copy(rowt[s][0:66, :], bank[bk][0:66, :]), "yT", ns=520)
                bank_free[bk] = (t,)
                wait("pe", t)
                bk = take_bank(s)
                for i in range(NBLK):
                    t = emit("pe", lambda e, bk=bk, i=i: e.transpose(
                        bank[bk][:, i * 66:(i + 1) * 66], rowt[s][0:66, i * 128:(i + 1) * 128], ident[0:66, 0:66]),
                        "yTT", ns=TR_NS)
                rowt_free[s] = (t,)
                ov = bank[bk][:, 0:264].rearrange("p (i n) -> p i n", n=66)
                wait("dve", t)
                t = emit("dve", lambda e, ov=ov, h=h: e.tensor_scalar(m["D"][:, h, :], ov[:, :, 64], TINY, None,
                                                                      ALU.max), "D", ns=130)
                wait("dve", t)
                t = emit("dve", lambda e, h=h: e.reciprocal(m["rD"][:, h, :], m["D"][:, h, :]), "rD", ns=70)
                rb = m["rD"][:, h, :].rearrange("p (i o) -> p i o", o=1).broadcast_to([128, NBLK, 64])
                y = X[s][0][:, h % 2, 0:256].rearrange("p (i n) -> p i n", n=64)
                ex = X[s][0][:, h % 2, 256:512].rearrange("p (i n) -> p i n", n=64)
                xh = x[:, :, h * 64:(h + 1) * 64]
                if h < 2:
                    wait("dve", *raw_free[s])
                wait("dve", t)
                t = emit("dve", lambda e, y=y, ov=ov, rb=rb: e.tensor_tensor(y, ov[:, :, 0:64], rb, ALU.mult),
                         "y0", ns=d_ns(256, True))
                bank_free[bk] = (t,)
                wait("act", t)
                te = emit("act", lambda e, y=y, ex=ex: e.activation(ex, y, ACT.Exp), "e0", ns=307)
                wait("dve", t)
                t = emit("dve", lambda e, y=y, xh=xh: e.scalar_tensor_tensor(xh, y, 0.0, xh, ALU.max, ALU.add),
                         "x0", ns=d_ns(256))
                wait("dve", te)
                t2 = emit("dve", lambda e, ex=ex: e.tensor_scalar(ex, ex, 1.0, -1.0, ALU.min, ALU.add), "m0",
                          ns=d_ns(128))
                wait("dve", t, t2)
                t = emit("dve", lambda e, ex=ex, xh=xh: e.tensor_tensor(xh, xh, ex, ALU.add), "x0b",
                         ns=d_ns(256))
            raw_free[s] = (t,)
            hw_free[s] = (t_att,)
            t_layer[0, b] = (t,)

        def layer1a(b):
            s, x, o = b % LANES, xs[b % XSLOTS], oT
            m = sm[s]
            ta, tb = X[s]
            t_h = layer_norm(s, x, t_layer[0, b])
            wait("pe", t_h, *t_w["m1"])
            wait("act", t_bias)
            for fo in range(4):
                bk = take_bank(s)
                cols = slice(fo * 128, (fo + 1) * 128)
                for k in range(2):
                    tp = mm3(bank[bk][:, :], (WM1["hi"][:, k, cols], WM1["lo"][:, k, cols]),
                             (hT[s]["hi"][:, k, :], hT[s]["lo"][:, k, :]), k == 0, k == 1, "m1")
                st = X[s][fo // 2][:, fo % 2, :]
                wait("act", tp, *(raw_free[s] if fo < 2 else st_free_of[s][fo - 2]))
                t = emit("act", lambda e, bk=bk, fo=fo, st=st: e.activation(
                    st, bank[bk][:, :], ACT.Relu, bias=b1[:, fo:fo + 1]), "m1", ns=a_ns(512, 1))
                bank_free[bk] = (t,)
                wait("act", t, *oT_free)
                t = emit("act", lambda e, fo=fo, st=st: e.copy(o["hi"][:, fo, :], st), "o1hi", ns=520)
                wait("pool", t, *oT_free)
                t_o = emit("pool", lambda e, fo=fo, st=st: e.tensor_tensor(
                    o["lo"][:, fo, :], st, f32(o["hi"][:, fo, :]), ALU.subtract), "o1lo", ns=1225)
                if fo == 1:
                    raw_free[s] = (t_o,)
                elif fo > 1:
                    st_free_of[s][fo - 2] = (t_o,)
            P_free[s] = [(tp,)] * NBLK
            t_raw, _ = project_raw(s, o, WFC, (t_o, *t_w["fc"]), 256)
            t_E = scores(s, t_raw, 0.2, 1)
            row = row_of(s, m["E"][:, 2, 0, :], t_E)
            t_P = build_P(s, 0, None, t_E, row)
            hw = hws[s]
            t_c = weight_columns(m["E"][:, 0, 0, :], wdf[s]["hi"][:, :], wdf[s]["lo"][:, :], t_E, hw_free[s])
            t_hw = scale_split(s, t_E, hw, hw_free[s])

            def attend_f(fo):
                bk = take_bank(s)
                fc = slice((fo % 2) * 128, (fo % 2 + 1) * 128)
                for j in range(NBLK):
                    tt = mm3(bank[bk][:, :], (hw["hi"][:, j, fc], hw["lo"][:, j, fc]),
                             (P[s]["hi"][:, j, :], P[s]["lo"][:, j, :]), j == 0, j == NBLK - 1, "attf")
                return bk, tt

            def post_y(fo, f):
                bk, t_at = f
                q = fo % 2
                wait("dve", t_at, t_rr, *raw_free[s])
                ty = emit("dve", lambda e: e.tensor_tensor(ta[:, q, :], bank[bk][:, :], rrow[:, :], ALU.mult),
                          "yf", ns=602)
                bank_free[bk] = (ty,)
                wait("act", ty, *st_free_of[s][q])
                te = emit("act", lambda e: e.activation(tb[:, q, :], ta[:, q, :], ACT.Exp), "ef", ns=520)
                return ty, te

            def post_pair(fos, t_e, t_proj):
                pair = [(n, fo, ta[:, fo % 2, :], tb[:, fo % 2, :]) for n, fo in enumerate(fos)]
                t = [None, None]
                for n, fo, y, ex in pair:
                    wait("dve", t_e[n])
                    t[n] = emit("dve", lambda e, ex=ex: e.tensor_scalar(ex, ex, 1.0, None, ALU.min), "mf",
                                ns=d_ns(256))
                for n, fo, y, ex in pair:
                    wait("act", t[n])
                    t[n] = emit("act", lambda e, ex=ex: e.activation(ex, ex, ACT.Exp, bias=minus1[:, 0:1]),
                                "ef2", ns=580)
                for n, fo, y, ex in pair:
                    wait("dve", t[n])
                    t[n] = emit("dve", lambda e, y=y, ex=ex: e.scalar_tensor_tensor(
                        y, y, 0.0, ex, ALU.max, ALU.add), "gf", ns=602)
                for n, fo, y, ex in pair:
                    wait("pool", t[n])
                    t[n] = emit("pool", lambda e, fo=fo, ex=ex: e.tensor_tensor(
                        ex, f32(o["hi"][:, fo, :]), f32(o["lo"][:, fo, :]), ALU.add), "resf", ns=1225)
                for n, fo, y, ex in pair:
                    wait("dve", t[n])
                    t[n] = emit("dve", lambda e, y=y, ex=ex: e.scalar_tensor_tensor(
                        y, y, -1.0, ex, ALU.add, ALU.add), "o2", ns=602)
                td = t[1]
                for n, fo, y, ex in pair:
                    wait("act", t[n], t_proj)
                    t[n] = emit("act", lambda e, fo=fo, y=y: e.copy(o["hi"][:, fo, :], y), "o2hi", ns=520)
                for n, fo, y, ex in pair:
                    wait("pool", t[n], t_proj)
                    t[n] = emit("pool", lambda e, fo=fo, y=y: e.tensor_tensor(
                        o["lo"][:, fo, :], y, f32(o["hi"][:, fo, :]), ALU.subtract), "o2lo", ns=1225)
                raw_free[s] = (t[1],)
                st_free_of[s] = [(td,), (td,)]
                return t[1]

            wait("pe", t_c)
            bk = take_bank(s)
            for j in range(NBLK):
                wait("pe", t_P[j])
                t = mm3(bank[bk][:, :], tuple(wdf[s][p][:, j:j + 1].broadcast_to([128, 128]) for p in PARTS2),
                        (P[s]["hi"][:, j, :], P[s]["lo"][:, j, :]), j == 0, j == NBLK - 1, "Df")
            rrow = rowt[s]
            wait("act", t, *rowt_free[s])
            t = emit("act", lambda e, bk=bk: e.copy(rrow[0:1, :], bank[bk][0:1, :]), "rrow", ns=520)
            bank_free[bk] = (t,)
            wait("pe", t)
            bk = take_bank(s)
            for i in range(NBLK):
                t = emit("pe", lambda e, bk=bk, i=i: e.transpose(
                    bank[bk][:, i:i + 1], rrow[0:1, i * 128:(i + 1) * 128], ident[0:1, 0:1]), "Df", ns=TR_NS)
            wait("dve", t)
            t_rd = emit("dve", lambda e, bk=bk: e.reciprocal(m["rD"][:, 0, :], bank[bk][:, 0:NBLK]), "rD", ns=130)
            bank_free[bk] = (t_rd,)
            bk, t = row_of(s, m["rD"][:, 0, :], t_rd)
            wait("act", t)
            t_rr = emit("act", lambda e, bk=bk: e.copy(rrow[:, :], bank[bk][:, :]), "rrow", ns=520)
            bank_free[bk] = (t_rr,)
            wait("pe", t_hw)
            f2, f3 = attend_f(2), attend_f(3)
            hw_free[s] = (f3[1],)
            te = [post_y(2, f2)[1], post_y(3, f3)[1]]
            t_hw, t_proj = project_scaled(s, o, WFC, t_E, hw, hw_free[s], slice(0, 256))
            post_pair((2, 3), te, t_proj)
            wait("pe", t_hw)
            f2, f3 = attend_f(0), attend_f(1)
            hw_free[s] = (f3[1],)
            P_free[s] = [(f3[1],)] * NBLK
            y2, y3 = post_y(0, f2), post_y(1, f3)
            rowt_free[s] = (y3[0],)
            t_layer["1a", b] = (post_pair((0, 1), (y2[1], y3[1]), t_proj),)

        def layer1b(b):
            nonlocal oT_free, rT_free
            s, x, o = b % LANES, xs[b % XSLOTS], oT
            m = sm[s]
            ta, tb = X[s]
            tA, tB = blocks(ta), blocks(tb)
            wait("pe", *t_layer["1a", b], *t_w["m2"])
            wait("act", t_bias)
            for fo in range(2):
                bk = take_bank(s)
                cols = slice(fo * 128, (fo + 1) * 128)
                for k in range(4):
                    tp = mm3(bank[bk][:, :], (WM2["hi"][:, k, cols], WM2["lo"][:, k, cols]),
                             (o["hi"][:, k, :], o["lo"][:, k, :]), k == 0, k == 3, "m2")
                wait("act", tp, *raw_free[s])
                t = emit("act", lambda e, bk=bk, fo=fo: e.activation(
                    ta[:, fo, :], bank[bk][:, :], ACT.Relu, bias=b2[:, fo:fo + 1]), "m2", ns=a_ns(512, 1))
                bank_free[bk] = (t,)
                wait("act", t, *rT_free)
                t_hs = emit("act", lambda e, fo=fo: e.activation(
                    rT["hi"][:, fo, :], ta[:, fo, :], ACT.Copy, accum_out=m["hs"][:, fo:fo + 1]), "o3hi",
                    ns=580)
                wait("pool", t_hs, *rT_free)
                t_o = emit("pool", lambda e, fo=fo: e.tensor_tensor(
                    rT["lo"][:, fo, :], ta[:, fo, :], f32(rT["hi"][:, fo, :]), ALU.subtract), "o3lo",
                    ns=1225)
            oT_free = (tp,)
            raw_free[s] = (t_o,)
            t_S = column_sums(s, WHA, t_hs)

            def evacuate(i, bk, td):
                wait("act", td, *raw_free[s])
                t = emit("act", lambda e: e.activation(
                    tA[:, i, :], bank[bk][:, 0:256], ACT.Copy, scale=m["rD"][:, 0, i:i + 1]), "yh", ns=358)
                wait("dve", t, t_S)
                t_y.append(emit("dve", lambda e: e.scalar_tensor_tensor(
                    tA[:, i, :], m["Sb"][:, :], empty["gt"][:, i:i + 1], tA[:, i, :], ALU.mult, ALU.add), "yh2",
                    ns=396))
                return (t,)

            t_y = []
            gat256(s, rT, WHA, (t_o, *t_w["ha"]), 0.2, maskT["gt"], evacuate)
            rbanks = []
            for bp in range(2):
                bk = take_bank(s)
                for bb in range(2):
                    for k in range(2):
                        out = bank[bk][:, bb * 256 + k * 128:bb * 256 + (k + 1) * 128]
                        cols = slice((2 * bp + bb) * 128, (2 * bp + bb + 1) * 128)
                        for p in PARTS2:
                            tr = emit("pe", lambda e, out=out, k=k, cols=cols, p=p,
                                      st=(bb == 0 and k == 0 and p == "hi"):
                                      e.matmul(out, rT[p][:, k, cols], identr[:, :], start=st,
                                               stop=(p == "lo"), skip_group_check=True),
                                      "r3" if (bb, k, p) == (1, 1, "lo") else None, ns=54)
                rbanks.append((bk, tr))
            rT_free = (tr,)
            te, tm = [None, None], [None, None]
            for h in range(2):
                wait("act", t_y[2 * h + 1], *st_free_of[s][h])
                te[h] = emit("act", lambda e, h=h: e.activation(tb[:, h, :], ta[:, h, :], ACT.Exp), "eh", ns=520)
            for h in range(2):
                wait("dve", te[h])
                tm[h] = emit("dve", lambda e, h=h: e.tensor_scalar(tb[:, h, :], tb[:, h, :], 1.0, None, ALU.min),
                             "mh", ns=d_ns(256))
            for h in range(2):
                wait("act", tm[h])
                te[h] = emit("act", lambda e, h=h: e.activation(tb[:, h, :], tb[:, h, :], ACT.Exp,
                                                                bias=minus1[:, 0:1]), "eh2", ns=580)
            for h in range(2):
                wait("dve", te[h])
                tm[h] = emit("dve", lambda e, h=h: e.scalar_tensor_tensor(
                    ta[:, h, :], ta[:, h, :], 0.0, tb[:, h, :], ALU.max, ALU.add), "gh", ns=602)
            for h in range(2):
                bk, tr = rbanks[h]
                wait("dve", tm[h], tr)
                tm[h] = emit("dve", lambda e, h=h, bk=bk: e.scalar_tensor_tensor(
                    ta[:, h, :], ta[:, h, :], -1.0, bank[bk][:, :], ALU.add, ALU.add), "gh2", ns=662)
                bank_free[bk] = (tm[h],)
            for h in range(2):
                wait("dve", tm[h])
                xv = x[:, 2 * h:2 * h + 2, :].rearrange("p a n -> p (a n)")
                t = emit("dve", lambda e, h=h, xv=xv: e.scalar_tensor_tensor(
                    xv, ta[:, h, :], 0.0, xv, ALU.max, ALU.add), "xh", ns=602)
            raw_free[s] = (t,)
            st_free_of[s] = [(t,), (t,)]
            t_layer["1b", b] = (t,)

        def layer2(b):
            s, x = b % LANES, xs[b % XSLOTS]
            m = sm[s]
            ta, tb = X[s]
            tA, tB = blocks(ta), blocks(tb)
            t_h = layer_norm(s, x, t_layer["1b", b])
            t_e = []

            def evacuate(i, bk, td):
                wait("act", td, *raw_free[s], *st_free_of[s][0], *st_free_of[s][1])
                emit("act", lambda e: e.activation(
                    tA[:, i, :], bank[bk][:, 0:256], ACT.Relu, scale=m["rD"][:, 0, i:i + 1]), "rl2", ns=358)
                t = emit("act", lambda e: e.activation(
                    tB[:, i, :], bank[bk][:, 0:256], ACT.Exp, scale=m["rD"][:, 0, i:i + 1]), "e2", ns=358)
                t_e.append(t)
                return (t,)

            gat256(s, hT[s], W2, (t_h, *t_w["L2"]), 0.2, maskT["self"], evacuate)
            tg = [None, None]
            for h in range(2):
                wait("dve", t_e[2 * h + 1])
                tg[h] = emit("dve", lambda e, h=h: e.scalar_tensor_tensor(
                    ta[:, h, :], tb[:, h, :], 1.0, ta[:, h, :], ALU.min, ALU.add), "g2", ns=602)
            for h in range(2):
                wait("dve", tg[h])
                xv = x[:, 2 * h:2 * h + 2, :].rearrange("p a n -> p (a n)")
                t = emit("dve", lambda e, h=h, xv=xv: e.scalar_tensor_tensor(
                    xv, ta[:, h, :], -1.0, xv, ALU.add, ALU.add), "x2", ns=602)
            raw_free[s] = (t,)
            st_free_of[s] = [(t,), (t,)]
            t_layer[2, b] = (t,)

        t_store = {}

        def layer3(b):
            s, x = b % LANES, xs[b % XSLOTS]
            m = sm[s]
            ta = X[s][0]
            tA = blocks(ta)
            t_h = layer_norm(s, x, t_layer[2, b])
            wait("dve", t_h)
            t_S = column_sums(s, W3, t_h)
            t_y = []

            def evacuate(i, bk, td):
                wait("act", td, *raw_free[s])
                t = emit("act", lambda e: e.activation(
                    tA[:, i, :], bank[bk][:, 0:256], ACT.Copy, scale=m["rD"][:, 0, i:i + 1]), "y3", ns=358)
                wait("dve", t, t_S)
                t_y.append(emit("dve", lambda e: e.scalar_tensor_tensor(
                    tA[:, i, :], m["Sb"][:, :], empty["ne"][:, i:i + 1], tA[:, i, :], ALU.mult, ALU.add), "y32",
                    ns=396))
                return (t,)

            gat256(s, hT[s], W3, (t_h, *t_w["L3"]), 0.01, maskT["ne"], evacuate)
            for h in range(2):
                wait("dve", t_y[2 * h + 1])
                xv = x[:, 2 * h:2 * h + 2, :].rearrange("p a n -> p (a n)")
                t = emit("dve", lambda e, h=h, xv=xv: e.scalar_tensor_tensor(
                    xv, ta[:, h, :], 0.0, xv, ALU.max, ALU.add), "x3", ns=602)
            raw_free[s] = (t,)
            wait("sp", t)
            t_store[b] = emit("sp", lambda e: e.dma_start(o_v[b], x[:, :, :]), f"out{b % XSLOTS}", ns=3000, by=16)
            x_free[b % XSLOTS] = (t_store[b],)

        for b in range(B):
            if b:
                L.lane, L.rank = "X", b
                load_x(b)
            L.lane, L.rank = f"L{b % LANES}", b
            for stage in (layer0, layer1a, layer1b, layer2, layer3):
                stage(b)
        for b in range(max(0, B - XSLOTS), B):
            L.pending.setdefault(("end", "sp"), []).append(t_store[b])
        ends = L.pending.pop(("end", "sp"))
        order = L.merge()
        L.pending[("end", "sp")] = ends

        block = ctx.enter_context(nc.Block())

        @block.sync
        def _(e):
            L.play("sp", order, e)

        @block.tensor
        def _(e):
            L.play("pe", order, e)

        @block.vector
        def _(e):
            L.play("dve", order, e)

        @block.scalar
        def _(e):
            L.play("act", order, e)

        @block.gpsimd
        def _(e):
            L.play("pool", order, e)


_INS = ["x", "adj", "L0_gnn_W", "L0_gnn_a", "L1_gnn_mlp1_w", "L1_gnn_mlp1_b", "L1_gnn_mlp2_w", "L1_gnn_mlp2_b",
        "L1_gnn_W_fc", "L1_gnn_a_fc", "L1_gnn_W_hand", "L1_gnn_a_hand", "L2_gnn_W", "L2_gnn_a", "L3_gnn_W",
        "L3_gnn_a"]


def kernel(**inputs):
    import numpy as _np
    import concourse.bacc as _bacc
    from concourse import mybir as _mybir
    from concourse.bass_utils import run_bass_kernel_spmd as _run

    nc = _bacc.Bacc("TRN2", target_bir_lowering=False, num_devices=1)
    arrays, args = {}, []
    for name in _INS:
        a = _np.ascontiguousarray(inputs[name])
        arrays[f"in_{name}_dram"] = a
        args.append(nc.dram_tensor(f"in_{name}_dram", a.shape, _mybir.dt.from_np(a.dtype), kind="ExternalInput").ap())
    args.append(nc.dram_tensor("out_0_dram", (B, N, F), F32, kind="ExternalOutput").ap())
    build(nc, *args)
    r = _run(nc, [arrays], core_ids=[0])
    return r.results[0]["out_0_dram"]
```

```python
from contextlib import ExitStack

import concourse.bass as bass
from concourse import mybir

ALU = mybir.AluOpType
ACT = mybir.ActivationFunctionType
F32 = mybir.dt.float32
F32R = mybir.dt.float32r
I32 = mybir.dt.int32
U8 = mybir.dt.uint8
AXX = mybir.AxisListType.X

B, N, F = 32, 512, 256
NBLK = 4
TINY = 1e-37
EPS = 1e-5
SHIFT = 30.0
LANES = 3
LANE_BANKS = {0: (0, 1, 2), 1: (3, 4), 2: (5, 6), 3: (5, 6)}
XSLOTS = 4


class Queues:

    PARTS = ("pe", "dve", "act", "pool", "sp")

    def __init__(self, nc, ctx):
        self.nc, self.ctx = nc, ctx
        self.q, self.sems, self.count = {}, {}, {}
        self.lane = "I"
        self.pending = {}
        self.rank = 0

    def emit(self, part, fn, sig=None, ns=60, by=1):
        waits = self.pending.pop((self.lane, part), [])
        token = None
        if sig is not None:
            name = f"{part}_{self.lane}_{STAGE_OF.get(sig, sig)}"
            if name not in self.sems:
                self.sems[name] = self.ctx.enter_context(self.nc.semaphore(name))
                self.count[name] = 0
            self.count[name] += by
            token = (name, self.count[name])
        self.q.setdefault((self.lane, part), []).append((fn, waits, token, by, ns, self.rank))
        return token

    def wait(self, part, *tokens):
        self.pending.setdefault((self.lane, part), []).extend(tokens)

    def bursts(self):
        start = {}
        for lane in {lane for lane, _ in self.q}:
            at = {part: 0 for part in self.PARTS if (lane, part) in self.q}
            free, done = dict.fromkeys(at, 0.0), {}
            moved = True
            while moved:
                moved = False
                for part in at:
                    queue = self.q[(lane, part)]
                    while at[part] < len(queue):
                        _, waits, token, _, ns, _ = queue[at[part]]
                        own = [w for w in waits if w[0].split("_")[1] == lane]
                        if not all(w in done for w in own):
                            break
                        t = max([free[part]] + [done[w] + LAT[w[0].split("_")[0], part] for w in own])
                        start[(lane, part, at[part])] = t
                        free[part] = t + ns
                        if token is not None:
                            done[token] = free[part]
                        at[part] += 1
                        moved = True
        rest = {}
        for (lane, part), queue in self.q.items():
            left = 0.0
            for n in range(len(queue) - 1, -1, -1):
                key = (lane, part, n)
                if n + 1 < len(queue) and start[(lane, part, n + 1)] - start[key] - queue[n][4] > PAUSE:
                    left = 0.0
                left += queue[n][4]
                rest[key] = left
        return rest

    def merge(self):
        assert not any(self.pending.values())
        rest = self.bursts()
        at = {k: 0 for k in self.q}
        free = dict.fromkeys(self.PARTS, 0.0)
        done = {}
        ready = {}
        order = {p: [] for p in self.PARTS}
        left = sum(len(v) for v in self.q.values())
        while left:
            best = {}
            for (lane, part), n in at.items():
                queue = self.q[(lane, part)]
                if n == len(queue):
                    continue
                key = (lane, part, n)
                if key not in ready:
                    waits = queue[n][1]
                    if not all(w in done for w in waits):
                        continue
                    ready[key] = max([done[w] + LAT[w[0].split("_")[0], part] for w in waits], default=0.0)
                start = max(free[part], ready[key])
                rank = (start, 0 if part == "pool" else rest[key], queue[n][5])
                if part not in best or rank < best[part][0]:
                    best[part] = (rank, lane)
            assert best, "the lanes wait for each other"
            part = min(best, key=lambda p: best[p][0][0])
            (start, _, _), lane = best[part]
            item = self.q[(lane, part)][at[(lane, part)]]
            at[(lane, part)] += 1
            left -= 1
            if part == "pe" and free[part] and start - free[part] > IDLE:
                order[part] += [(self.idle, (), None, 0, 213, 0)] * int((start - free[part]) * FILL / 213)
            free[part] = start + (50 if part == "sp" else item[4])
            if item[2] is not None:
                done[item[2]] = start + item[4]
            order[part].append(item)
        return order

    def play(self, part, order, eng):
        seen = {}
        for fn, waits, token, by, _, _ in order[part]:
            for name, value in waits:
                if seen.get(name, 0) < value:
                    seen[name] = value
                    eng.wait_ge(self.sems[name], value)
            ins = fn(eng)
            if token is not None:
                ins.then_inc(self.sems[token[0]], by)
        for name, value in self.pending.pop(("end", part), []):
            eng.wait_ge(self.sems[name], value)


PAUSE = 400
IDLE, FILL = 700, 0.8

STAGE_OF = {sig: stage for stage, sigs in {
    "norm": ("st", "mv", "ve", "rs", "hn", "hT", "hThi", "hTlo"),
    "score": ("sc", "tm", "TM", "T", "u", "u1", "u2", "E"),
    "sums": ("hs", "S", "Sb"),
    "P": ("row", "P", "Phi", "Plo"),
    "hw": ("h", "raw", "hwf", "hwhi", "hwlo", "hwhi0", "hwlo0", "wch", "wcl"),
    "mlp": ("m1", "m2", "o1hi", "o1lo", "o3hi", "o3lo"),
    "att": ("att", "att0", "attf", "Df", "D", "rD", "rrow"),
    "post": ("yT", "yTT", "y0", "e0", "x0", "m0", "x0b", "yf", "ef", "mf", "ef2", "gf", "resf", "o2", "o2hi", "o2lo",
             "yh", "yh2", "eh", "mh", "eh2", "gh", "gh2", "xh", "r3", "e2", "g2", "x2", "y3", "y32", "x3"),
    "load": ("whi", "wlo", "wT", "wTe", "wA", "wAh", "wAl", "az"),
    "mask": ("mrow", "emp", "mT", "mTe", "emp2", "self", "mask"),
}.items() for sig in sigs}

LAT = {(a, b): {"pe": 200, "dve": 120, "act": 145, "pool": 115, "sp": 1500}[a] + {"pe": 80, "act": 10}.get(b, 0)
       for a in Queues.PARTS for b in Queues.PARTS}
LAT.update({(a, a): 60 for a in Queues.PARTS})
LAT["pool", "dve"] = 70


def build(nc, x_d, adj_d, L0_W, L0_a, m1_w, m1_b, m2_w, m2_b, fc_w, fc_a, ha_w, ha_a, L2_W, L2_a, L3_W, L3_a, out_d):
    ctx = ExitStack()
    with ctx:
        def sb(name, shape, dt=F32):
            return ctx.enter_context(nc.sbuf_tensor(name, shape, dt))

        L = Queues(nc, ctx)
        emit, wait = L.emit, L.wait

        bank = [ctx.enter_context(nc.psum_tensor(f"bank{i}", [128, 512], F32)) for i in range(8)]
        bank_free = [() for _ in range(8)]
        turn = {0: 0, 1: 0, 2: 0, 3: 0}

        identr = sb("identr", [128, 128], F32R)
        ident = identr[:, :].bitcast(F32)
        kshift = sb("kshift", [128, 1])
        minus1 = sb("minus1", [128, 1])
        mhalf = sb("mhalf", [128, NBLK])
        maskT = {k: sb(f"mask_{k}", [128, NBLK, N], U8) for k in ("ne", "gt", "self")}
        empty = {k: sb(f"empty_{k}", [128, NBLK]) for k in ("ne", "gt")}
        b1 = sb("b1", [128, 4])
        b2 = sb("b2", [128, 2])

        def weights(name, kb, fo, nq):
            return {"hi": sb(name + "_hi", [128, kb, fo + nq], F32R),
                    "lo": sb(name + "_lo", [128, kb, fo + nq], F32R), "kb": kb, "fo": fo, "nq": nq}

        W0 = weights("w0", 2, 256, 8)
        WM1 = weights("wm1", 2, 512, 0)
        WFC = weights("wfc", 4, 512, 2)
        WM2 = weights("wm2", 4, 256, 0)
        WHA = weights("wha", 2, 256, 2)
        W2 = weights("w2", 2, 256, 2)
        W3 = weights("w3", 2, 256, 2)

        PARTS2 = ("hi", "lo")
        xs = [sb(f"x{i}", [128, NBLK, F]) for i in range(XSLOTS)]
        raw = [sb(f"raw{s}", [128, NBLK, 264]) for s in range(LANES)]
        X = [[raw[s][:, :, :].rearrange("p b n -> p (b n)")[:, 0:1024].rearrange("p (a n) -> p a n", a=2),
              sb(f"X{s}", [128, 2, 512])[:, :, :]] for s in range(LANES)]
        P = [{p: sb(f"P{s}{p}", [128, NBLK, N], F32R) for p in PARTS2} for s in range(LANES)]
        hT = [{p: P[s][p][:, 0:2, :] for p in PARTS2} for s in range(LANES)]
        oT = {p: sb(f"oT{p}", [128, 4, N], F32R) for p in PARTS2}
        rT = {p: sb(f"rT{p}", [128, 2, N], F32R) for p in PARTS2}
        hws = [{p: sb(f"hw{s}{p}", [128, NBLK, 264], F32R) for p in PARTS2} for s in range(LANES)]
        wdf = [{p: sb(f"wdf{s}{p}", [128, NBLK], F32R) for p in PARTS2} for s in range(LANES)]
        rowt = [sb(f"rowt{s}", [128, N]) for s in range(LANES)]
        NH = 4
        sm = [{
            "st": sb(f"st{s}", [128, NBLK, 6]), "mv": sb(f"mv{s}", [128, NBLK, 2]),
            "ve": sb(f"ve{s}", [128, NBLK]), "rs": sb(f"rs{s}", [128, NBLK]),
            "tm": sb(f"tm{s}", [128, NH]),
            "T": sb(f"T{s}", [128, NH]), "A": sb(f"A{s}", [128, 3, NH, NBLK]),
            "E": sb(f"E{s}", [128, 3, NH, NBLK]),
            "D": sb(f"D{s}", [128, NH, NBLK]), "rD": sb(f"rD{s}", [128, NH, NBLK]),
            "hs": sb(f"hs{s}", [128, 2]), "hsr": sb(f"hsr{s}", [128, 2, 2], F32R),
            "Sb": sb(f"Sb{s}", [128, F]),
        } for s in range(LANES)]

        P_free = [[()] * NBLK for _ in range(LANES)]
        raw_free = [()] * LANES
        st_free_of = [[(), ()] for _ in range(LANES)]
        hw_free = [()] * LANES
        rowt_free = [()] * LANES
        oT_free = ()
        rT_free = ()
        x_free = [()] * XSLOTS

        def take_bank(s):
            ring = LANE_BANKS[s]
            i = ring[turn[s] % len(ring)]
            turn[s] += 1
            assert bank_free[i] is not None
            wait("pe", *bank_free[i])
            bank_free[i] = None
            return i

        def f32(ap):
            return ap.bitcast(F32)

        def d_ns(n, psum=False):
            return (130 if psum else 65) + 1.04 * n

        def a_ns(n, ptr=0):
            return (144 if ptr else 52 if n < 280 else 94) + 0.83 * n

        def p_ns(n):
            return 60 + 2.2 * n

        TR_NS = 107

        L.lane, L.rank = "I", -1
        id_st = X[2][1][:, 0, 0:128]
        t0 = emit("pool", lambda e: e.memset(id_st, 0.0), "c0")
        wait("pool", t0)
        t0 = emit("pool", lambda e: e.affine_select(out=id_st, in_=id_st, compare_op=ALU.not_equal,
                                                      fill=1.0, base=0, pattern=[[-1, 128]],
                                                      channel_multiplier=1), "id")
        emit("pool", lambda e: e.memset(kshift[:, :], SHIFT))
        emit("pool", lambda e: e.memset(minus1[:, :], -1.0))
        t_const = emit("pool", lambda e: e.memset(mhalf[:, :], -0.5), "const")
        wait("dve", t0)
        t_id = emit("dve", lambda e: e.tensor_copy(identr[:, :], id_st), "idr")

        x_v = x_d.rearrange("n (p b) f -> n p b f", b=NBLK)
        o_v = out_d.rearrange("n (p b) f -> n p b f", b=NBLK)
        t_x = {}

        def load_x(b):
            wait("sp", *x_free[b % XSLOTS])
            t_x[b] = emit("sp", lambda e: e.dma_start(xs[b % XSLOTS][:, :, :], x_v[b]), f"xin{b % XSLOTS}",
                          ns=3000, by=16)

        load_x(0)

        wT = X[1][0]
        a_st = X[1][1][:, 0, 0:32].rearrange("p (k q) -> p k q", q=8)
        st_free = [[], [t_id]]
        misc = {"wT": (), "a": ()}

        def load_weights(w, w_d, a_fill):
            kb, fo, nq = w["kb"], w["fo"], w["nq"]
            wv = w_d.rearrange("(k p) n -> p k n", p=128)
            per = 1024 // fo
            tiles, toks, n_c = [], [], (kb + per - 1) // per
            for c in range(n_c):
                k0, k1 = c * per, min(kb, (c + 1) * per)
                dst = X[2][c].rearrange("p a n -> p (a n)")[:, 0:(k1 - k0) * fo].rearrange(
                    "p (k n) -> p k n", n=fo)
                wait("sp", *st_free[c])
                toks.append(emit("sp", lambda e, dst=dst, k0=k0, k1=k1: e.dma_start(dst, wv[:, k0:k1, :]),
                                 f"wl{c}", ns=3500, by=16))
                tiles += [dst[:, k, :] for k in range(k1 - k0)]
            ta_ = None
            if nq:
                wait("dve", *misc["a"])
                tz = emit("dve", lambda e: e.memset(a_st, 0.0), "az")
                wait("sp", tz)
                ta_ = a_fill()
            wait("act", *toks)
            for k in range(kb):
                th = emit("act", lambda e, k=k: e.copy(w["hi"][:, k, 0:fo], tiles[k]), "whi", ns=a_ns(fo))
            wait("dve", *toks, th)
            for k in range(kb):
                tl = emit("dve", lambda e, k=k: e.tensor_tensor(w["lo"][:, k, 0:fo], tiles[k], f32(w["hi"][:, k, 0:fo]),
                                                                ALU.subtract), "wlo", ns=d_ns(fo))
            free = [tl]
            if nq:
                ob = fo // 128
                wait("pe", *toks, ta_, t_id)
                for k in range(kb):
                    bk = take_bank(3)
                    for o in range(ob):
                        tw = emit("pe", lambda e, k=k, o=o, bk=bk: e.transpose(
                            bank[bk][:, o * 128:(o + 1) * 128], tiles[k][:, o * 128:(o + 1) * 128],
                            ident[:, :]), "wT", ns=TR_NS)
                    wait("dve", tw, *misc["wT"])
                    te = emit("dve", lambda e, bk=bk, ob=ob: e.tensor_copy(
                        wT[:, 0, 0:ob * 128], bank[bk][:, 0:ob * 128]), "wTe", ns=d_ns(ob * 128))
                    bank_free[bk] = (te,)
                    wait("pe", te)
                    bk = take_bank(3)
                    for o in range(ob):
                        tp = emit("pe", lambda e, o=o, bk=bk, ob=ob: e.matmul(
                            bank[bk][:, 0:nq], wT[:, 0, o * 128:(o + 1) * 128], a_st[:, o, 0:nq],
                            start=(o == 0), stop=(o == ob - 1)), "wA")
                    misc["wT"] = misc["a"] = (tp,)
                    wait("dve", tp)
                    te = emit("dve", lambda e, k=k, bk=bk: e.tensor_copy(w["hi"][:, k, fo:fo + nq], bank[bk][:, 0:nq]),
                              "wAh")
                    wait("dve", te)
                    te = emit("dve", lambda e, k=k, bk=bk: e.tensor_tensor(
                        w["lo"][:, k, fo:fo + nq], bank[bk][:, 0:nq], f32(w["hi"][:, k, fo:fo + nq]),
                        ALU.subtract), "wAl")
                    bank_free[bk] = (te,)
                free.append(tw)
            for c in range(n_c):
                st_free[c] = free
            return [tl] + ([te] if nq else [])

        def a_dma(dst, src):
            return emit("sp", lambda e: e.dma_start(dst, src, allow_slow_non_contiguous=True), "al", ns=2500, by=16)

        def fill_heads():
            for h in range(4):
                for t in range(2):
                    p0 = (h % 2) * 64
                    tok = a_dma(a_st[p0:p0 + 64, h // 2, t * 4 + h:t * 4 + h + 1],
                                L0_a[h, t * 64:(t + 1) * 64].rearrange("(p o) -> p o", o=1))
            return tok

        def fill_col(a_d, ob):
            def go():
                for t in range(2):
                    tok = a_dma(a_st[:, 0:ob, t],
                                a_d[t * ob * 128:(t + 1) * ob * 128, 0].rearrange("(k p) -> p k", p=128))
                return tok
            return go

        t_w = {}
        t_w["L0"] = load_weights(W0, L0_W, fill_heads)

        adj_v = adj_d.rearrange("(p b) j -> p b j", b=NBLK)
        wait("dve", *misc["wT"], *misc["a"])
        t_pe, t_red = (), ()
        for half in range(2):
            wait("sp", *st_free[half])
            src = X[2][half].bitcast(I32)
            t_adj = emit("sp", lambda e, src=src, half=half: e.dma_start(
                src, adj_v[:, 2 * half:2 * half + 2, :]), f"wl{half}", ns=3500, by=16)
            mrow = {"ne": X[1][0], "gt": X[1][1]}
            wait("dve", t_adj, *t_pe, *t_red)
            for k, op in (("ne", ALU.not_equal), ("gt", ALU.is_gt)):
                t_m = emit("dve", lambda e, k=k, op=op, src=src, mrow=mrow: e.tensor_scalar(
                    mrow[k][:, :, :], src, 0.0, None, op), "mrow", ns=d_ns(1024))
            st_free[half] = [t_m]
            wait("dve", t_m)
            for k in ("ne", "gt"):
                t_r = emit("dve", lambda e, k=k, half=half, mrow=mrow: e.tensor_reduce(
                    empty[k][:, 2 * half:2 * half + 2], mrow[k][:, :, :], AXX, ALU.max), "emp", ns=d_ns(1024))
            t_red = (t_r,)
            wait("pe", t_m, t_id)
            for k in ("ne", "gt"):
                for bj in range(NBLK):
                    bk = take_bank(3)
                    for b in range(2):
                        tp = emit("pe", lambda e, k=k, b=b, bj=bj, bk=bk, mrow=mrow: e.transpose(
                            bank[bk][:, b * 128:(b + 1) * 128], mrow[k][:, b, bj:N:NBLK], ident[:, :]), "mT",
                            ns=TR_NS)
                    wait("dve", tp)
                    t_ev = emit("dve", lambda e, k=k, bj=bj, bk=bk, half=half: e.tensor_copy(
                        maskT[k][:, bj, half * 256:(half + 1) * 256], bank[bk][:, 0:256]), "mTe", ns=d_ns(256))
                    bank_free[bk] = (t_ev,)
            t_pe = (tp,)
        misc["wT"] = misc["a"] = (tp, t_r)
        wait("dve", t_r)
        for k in ("ne", "gt"):
            t_emp = emit("dve", lambda e, k=k: e.tensor_scalar(empty[k][:, :], empty[k][:, :], -1.0, 1.0,
                                                               ALU.mult, ALU.add), "emp2")
        wait("dve", t_ev)
        t_cp = emit("dve", lambda e: e.tensor_copy(maskT["self"][:, :, :], maskT["gt"][:, :, :]), "self",
                    ns=d_ns(2048))
        wait("dve", t_cp)
        for bj in range(NBLK):
            t_mask = emit("dve", lambda e, bj=bj: e.tensor_tensor(
                maskT["self"][:, bj, bj * 128:(bj + 1) * 128], maskT["self"][:, bj, bj * 128:(bj + 1) * 128],
                ident[:, :], ALU.max), "mask", ns=d_ns(128))

        t_bias = emit("sp", lambda e: e.dma_start(b1[:, :], m1_b.rearrange("(k p) -> p k", p=128),
                                                  allow_slow_non_contiguous=True), "b", ns=2500, by=16)
        t_bias = emit("sp", lambda e: e.dma_start(b2[:, :], m2_b.rearrange("(k p) -> p k", p=128),
                                                  allow_slow_non_contiguous=True), "b", ns=2500, by=16)
        t_w["m1"] = load_weights(WM1, m1_w, None)
        t_w["fc"] = load_weights(WFC, fc_w, fill_col(fc_a, 4))
        t_w["m2"] = load_weights(WM2, m2_w, None)
        t_w["ha"] = load_weights(WHA, ha_w, fill_col(ha_a, 2))
        t_w["L2"] = load_weights(W2, L2_W, fill_col(L2_a, 2))
        t_w["L3"] = load_weights(W3, L3_W, fill_col(L3_a, 2))
        ended = tuple(st_free[0]) + tuple(st_free[1]) + misc["wT"]
        for s_ in (1, 2):
            raw_free[s_] = ended
            st_free_of[s_] = [ended, ended]

        def mm3(out, a, b, first, last, sig=None, group=True, n=512):
            t = None
            for q, (u, v) in enumerate(((a[0], b[0]), (a[0], b[1]), (a[1], b[0]))):
                st, sp = first and q == 0, last and q == 2
                t = emit("pe", lambda e, u=u, v=v, st=st, sp=sp: e.matmul(
                    out, u, v, start=st, stop=sp, skip_group_check=not group),
                    sig if (sp and sig) else None, ns=max(107, n / 2.4)) or t
            return t

        def block_stats(s, x, b, t_in):
            m = sm[s]
            wait("dve", *t_in)
            t = emit("dve", lambda e: e.bn_stats(m["st"][:, b, :], x[:, b, :]), "st", ns=335)
            wait("dve", t)
            return emit("dve", lambda e: e.bn_aggr(m["mv"][:, b, :], m["st"][:, b, :]), "mv", ns=75)

        def layer_norm(s, x, t_mv):
            t = rstd(s, t_mv)
            return normalize(s, x, t)

        def rstd(s, t_mv):
            m = sm[s]
            wait("dve", t_mv)
            t = emit("dve", lambda e: e.tensor_scalar(m["ve"][:, :], m["mv"][:, :, 1], EPS, None, ALU.add), "ve")
            wait("pool", t, t_const)
            t = emit("pool", lambda e: e.tensor_tensor(m["rs"][:, :], m["ve"][:, :], mhalf[:, :], ALU.pow), "rs",
                     ns=960)
            return t

        def normalize(s, x, t):
            m = sm[s]
            hn = X[s][0].rearrange("p a (b n) -> p (a b) n", n=256)
            wait("dve", t, *raw_free[s])
            t_hn = [emit("dve", lambda e, b=b: e.tensor_scalar(
                hn[:, b, :], x[:, b, :], m["mv"][:, b, 0:1], m["rs"][:, b:b + 1],
                ALU.subtract, ALU.mult), "hn", ns=323) for b in range(NBLK)]
            wait("pe", t_id)
            t_k = []
            for k in range(2):
                bk = take_bank(s)
                for b in range(NBLK):
                    wait("pe", t_hn[b])
                    t = emit("pe", lambda e, b=b, k=k, bk=bk: e.transpose(
                        bank[bk][:, b * 128:(b + 1) * 128], hn[:, b, k * 128:(k + 1) * 128], ident[:, :]), "hT",
                        ns=TR_NS)
                raw_free[s] = (t,)
                wait("act", t, *P_free[s][0])
                t = emit("act", lambda e, k=k, bk=bk: e.activation(
                    hT[s]["hi"][:, k, :], bank[bk][:, :], ACT.Relu, accum_out=m["hs"][:, k:k + 1]), "hThi",
                    ns=571)
                wait("dve", t, *P_free[s][0])
                t = emit("dve", lambda e, k=k, bk=bk: e.scalar_tensor_tensor(
                    hT[s]["lo"][:, k, :], bank[bk][:, :], 0.0, f32(hT[s]["hi"][:, k, :]),
                    ALU.max, ALU.subtract), "hTlo", ns=602)
                bank_free[bk] = (t,)
                t_k.append(t)
            return t_k

        def scores(s, t_raw, alpha, nh):
            m = sm[s]
            sc = raw[s][:, :, 256:256 + 2 * nh].rearrange("p b q -> p q b")
            wait("dve", t_raw)
            t = emit("dve", lambda e: e.tensor_reduce(m["tm"][:, 0:nh], sc[:, nh:2 * nh, :], AXX, ALU.max),
                     "tm", ns=80)
            wait("pe", t)
            bm = take_bank(s)
            for h in range(nh):
                t = emit("pe", lambda e, h=h: e.transpose(
                    bank[bm][:, h * 128:(h + 1) * 128], m["tm"][:, h:h + 1].broadcast_to([128, 128]),
                    ident[:, :]), "TM", ns=TR_NS)
            wait("dve", t)
            v2 = bank[bm][:, 0:nh * 128].rearrange("p (h n) -> p h n", h=nh)
            t = emit("dve", lambda e: e.tensor_reduce(m["T"][:, 0:nh], v2, AXX, ALU.max), "T",
                     ns=65 + 1.04 * 128 * nh)
            bank_free[bm] = (t,)
            wait("dve", t)
            Tb = m["T"][:, 0:nh].rearrange("p (h o) -> p h o", o=1).broadcast_to([128, nh, NBLK])
            t = emit("dve", lambda e: e.tensor_tensor(m["A"][:, 2, 0:nh, :], sc[:, 0:nh, :], Tb, ALU.add), "u")
            t_u = emit("dve", lambda e: e.tensor_tensor(m["A"][:, 0, 0:nh, :], sc[:, nh:2 * nh, :], Tb,
                                                        ALU.subtract), "u1")
            wait("dve", t)
            t = emit("dve", lambda e: e.tensor_scalar(m["A"][:, 2, 0:nh, :], m["A"][:, 2, 0:nh, :],
                                                      0.0, None, ALU.max), "u2")
            wait("act", t, t_const)
            for q, src, sc_ in ((2, 2, -(1.0 - alpha)), (1, 0, 1.0 - alpha), (0, 0, alpha)):
                if q == 1:
                    wait("act", t_u)
                t = emit("act", lambda e, q=q, src=src, sc_=sc_: e.activation(
                    m["E"][:, q, 0:nh, :], m["A"][:, src, 0:nh, :], ACT.Exp, bias=kshift[:, 0:1], scale=sc_), "E",
                    ns=200)
                if q == 2:
                    t_c = t
            return t_c, t

        def row_of(s, src, t_src):
            wait("pe", t_src)
            bk = take_bank(s)
            for b in range(NBLK):
                t = emit("pe", lambda e, b=b: e.transpose(
                    bank[bk][:, b * 128:(b + 1) * 128], src[:, b:b + 1].broadcast_to([128, 128]),
                    ident[:, :]), "row", ns=TR_NS)
            return bk, t

        def build_P(s, h, mask, t_E, row):
            m = sm[s]
            bk, t_row = row
            rowv = bank[bk][:, :]
            if mask is None:
                wait("act", t_row, *rowt_free[s])
                t_row = emit("act", lambda e: e.copy(rowt[s][:, :], bank[bk][:, :]), "row", ns=478)
                bank_free[bk] = (t_row,)
                rowv = rowt[s][:, :]
            out = []
            for j in range(NBLK):
                st = X[s][1][:, j % 2, :]
                wait("dve", t_row, t_E, *st_free_of[s][j % 2])
                r = m["E"][:, 1, h, j:j + 1]
                if mask is None:
                    t = emit("dve", lambda e, r=r, st=st: e.tensor_scalar(
                        st, rowv, r, None, ALU.max), "P", ns=340)
                    rowt_free[s] = (t,)
                else:
                    t = emit("dve", lambda e, j=j, r=r, st=st: e.scalar_tensor_tensor(
                        st, bank[bk][:, :], r, mask[:, j, :], ALU.max, ALU.mult), "P", ns=662)
                wait("act", t, *P_free[s][j])
                th = emit("act", lambda e, st=st, j=j: e.copy(P[s]["hi"][:, j, :], st), "Phi", ns=520)
                wait("pool", th, *P_free[s][j])
                tl = emit("pool", lambda e, st=st, j=j: e.tensor_tensor(
                    P[s]["lo"][:, j, :], st, f32(P[s]["hi"][:, j, :]), ALU.subtract), "Plo", ns=1225)
                st_free_of[s][j % 2] = (tl,)
                out.append(tl)
            if mask is not None:
                bank_free[bk] = (t,)
            return out

        def project_raw(s, src, w, t_src, f0):
            n = 256 + w["nq"]
            for b in range(NBLK):
                bk = take_bank(s)
                cols = slice(b * 128, (b + 1) * 128)
                for k in range(w["kb"]):
                    wait("pe", t_src[k])
                    tp = mm3(bank[bk][:, 0:n], (src["hi"][:, k, cols], src["lo"][:, k, cols]),
                             (w["hi"][:, k, f0:f0 + n], w["lo"][:, k, f0:f0 + n]), k == 0, k == w["kb"] - 1, "h",
                             n=n)
                wait("act", tp, *raw_free[s])
                t = emit("act", lambda e, b=b, bk=bk: e.copy(raw[s][:, b, 0:n], bank[bk][:, 0:n]), "raw",
                         ns=a_ns(n))
                bank_free[bk] = (t,)
            return t, tp

        def scale_split(s, t_E, hw, free):
            m = sm[s]
            for b in range(NBLK):
                wj = m["E"][:, 0, 0, b:b + 1]
                wait("act", t_E, *free)
                t = emit("act", lambda e, b=b, wj=wj: e.activation(
                    hw["hi"][:, b, 0:256], raw[s][:, b, 0:256], ACT.Copy, scale=wj), "hwhi", ns=400)
                wait("dve", t, *free)
                t = emit("dve", lambda e, b=b, wj=wj: e.scalar_tensor_tensor(
                    hw["lo"][:, b, 0:256], raw[s][:, b, 0:256], wj, f32(hw["hi"][:, b, 0:256]),
                    ALU.mult, ALU.subtract), "hwlo", ns=396)
            raw_free[s] = (t,)
            return t

        def project_scaled(s, src, w, t_E, hw, free, fs):
            m, kb = sm[s], w["kb"]
            for b in range(NBLK):
                bk = take_bank(s)
                cols = slice(b * 128, (b + 1) * 128)
                for k in range(kb):
                    tp = mm3(bank[bk][:, 0:256], (src["hi"][:, k, cols], src["lo"][:, k, cols]),
                             (w["hi"][:, k, fs], w["lo"][:, k, fs]), k == 0, k == kb - 1, "h", n=256)
                wj = m["E"][:, 0, 0, b:b + 1]
                wait("act", tp, t_E, *free)
                t = emit("act", lambda e, b=b, bk=bk, wj=wj: e.activation(
                    hw["hi"][:, b, 0:256], bank[bk][:, 0:256], ACT.Copy, scale=wj), "hwhi", ns=358)
                wait("dve", t, t_E, *free)
                t = emit("dve", lambda e, b=b, bk=bk, wj=wj: e.scalar_tensor_tensor(
                    hw["lo"][:, b, 0:256], bank[bk][:, 0:256], wj, f32(hw["hi"][:, b, 0:256]),
                    ALU.mult, ALU.subtract), "hwlo", ns=396)
                bank_free[bk] = (t,)
            return t, tp

        def weight_columns(src, hi, lo, t_E, free):
            wait("dve", t_E, *free)
            t = emit("dve", lambda e: e.tensor_copy(hi, src), "wch")
            wait("dve", t)
            return emit("dve", lambda e: e.tensor_tensor(lo, src, f32(hi), ALU.subtract), "wcl")

        def column_sums(s, w, t_hs):
            m = sm[s]
            wait("dve", t_hs)
            t = emit("dve", lambda e: e.tensor_copy(m["hsr"][:, :, 0], m["hs"][:, :]), "hs")
            wait("dve", t)
            t = emit("dve", lambda e: e.tensor_tensor(m["hsr"][:, :, 1], m["hs"][:, :], f32(m["hsr"][:, :, 0]),
                                                      ALU.subtract), "hs")
            wait("pe", t)
            bk = take_bank(s)
            for k in range(2):
                a = tuple(m["hsr"][:, k, p:p + 1].broadcast_to([128, 128]) for p in range(2))
                t = mm3(bank[bk][:, 0:256], a, (w["hi"][:, k, 0:256], w["lo"][:, k, 0:256]), k == 0, k == 1, "S", n=256)
            wait("act", t)
            t = emit("act", lambda e: e.activation(m["Sb"][:, :], bank[bk][:, 0:256], ACT.Copy, scale=1.0 / N),
                     "Sb", ns=a_ns(256))
            bank_free[bk] = (t,)
            return t

        def gat256(s, src, w, t_src, alpha, mask, evacuate):
            m = sm[s]
            t_raw, t_read = project_raw(s, src, w, t_src, 0)
            if src is hT[s]:
                P_free[s] = [(t_read,)] * NBLK
            t_c0, t_E = scores(s, t_raw, alpha, 1)
            row = row_of(s, m["E"][:, 2, 0, :], t_c0)
            t_P = build_P(s, 0, mask, t_E, row)
            hw, free = hws[s], hw_free[s]
            wc = m["E"][:, 0, 0, :].rearrange("p (b o) -> p b o", o=1).broadcast_to([128, NBLK, 2])
            t_c = weight_columns(wc, hw["hi"][:, :, 256:258], hw["lo"][:, :, 256:258], t_E, free)
            t_h = scale_split(s, t_E, hw, free)
            wait("pe", t_h, t_c)
            for i in range(NBLK):
                bk = take_bank(s)
                cols = slice(i * 128, (i + 1) * 128)
                for j in range(NBLK):
                    wait("pe", t_P[j])
                    t = mm3(bank[bk][:, 0:258], (P[s]["hi"][:, j, cols], P[s]["lo"][:, j, cols]),
                            (hw["hi"][:, j, 0:258], hw["lo"][:, j, 0:258]), j == 0, j == NBLK - 1, "att", n=258)
                wait("dve", t)
                td = emit("dve", lambda e, bk=bk, i=i: e.tensor_scalar(
                    m["D"][:, 0, i:i + 1], bank[bk][:, 256:257], TINY, None, ALU.max), "D", ns=66)
                wait("dve", td)
                td = emit("dve", lambda e, i=i: e.reciprocal(m["rD"][:, 0, i:i + 1], m["D"][:, 0, i:i + 1]), "rD",
                          ns=70)
                bank_free[bk] = evacuate(i, bk, td)
            P_free[s] = [(t,)] * NBLK
            hw_free[s] = (t,)

        def blocks(tile):
            return tile.rearrange("p a (b n) -> p (a b) n", n=256)

        t_layer = {}

        def layer0(b):
            s, x = b % LANES, xs[b % XSLOTS]
            m = sm[s]
            t_h = normalize(s, x, t_layer["rs", b])
            wait("pe", *t_w["L0"])
            t_raw, t_read = project_raw(s, hT[s], W0, t_h, 0)
            P_free[s] = [(t_read,)] * NBLK
            t_c0, t_E = scores(s, t_raw, 0.2, 4)
            hw, free = hws[s], hw_free[s]
            hv = {p: hw[p][:, :, :].rearrange("p b (h n) -> p b h n", n=66) for p in PARTS2}
            row = row_of(s, m["E"][:, 2, 0, :], t_c0)
            rv = raw[s][:, :, 0:256].rearrange("p b (h n) -> p b h n", n=64)
            wait("dve", t_E)
            for bl in range(NBLK):
                wb = m["E"][:, 0, :, bl:bl + 1].broadcast_to([128, 4, 64])
                t = emit("dve", lambda e, bl=bl, wb=wb: e.tensor_tensor(rv[:, bl], rv[:, bl], wb, ALU.mult), "hwf",
                         ns=d_ns(256))
            for bp in range(2):
                bs = slice(2 * bp, 2 * bp + 2)
                wait("act", t, *free)
                for bl in (2 * bp, 2 * bp + 1):
                    t1 = emit("act", lambda e, bl=bl: e.copy(hv["hi"][:, bl, :, 0:64], rv[:, bl]), "hwhi0", ns=307)
                wait("pool", t1, *free)
                for bl in (2 * bp, 2 * bp + 1):
                    t_hw = emit("pool", lambda e, bl=bl: e.tensor_tensor(
                        hv["lo"][:, bl, :, 0:64], rv[:, bl], f32(hv["hi"][:, bl, :, 0:64]), ALU.subtract),
                        "hwlo0", ns=687)
            raw_free[s] = (t_hw,)
            wait("dve", t_mask)
            t_P = build_P(s, 0, maskT["ne"], t_E, row)
            wc = m["E"][:, 0, :, :].rearrange("p h (b o) -> p b h o", o=1).broadcast_to([128, NBLK, 4, 2])
            t_c = weight_columns(wc, hv["hi"][:, :, :, 64:66], hv["lo"][:, :, :, 64:66], t_E, free)
            wait("pe", t_hw, t_c)
            y_free = raw_free[s]
            for h in range(4):
                if h < 3:
                    row = row_of(s, m["E"][:, 2, h + 1, :], t_E)
                bk = take_bank(s)
                for j in range(NBLK):
                    wait("pe", t_P[j])
                    t = mm3(bank[bk][0:66, :], (hv["hi"][:, j, h, :], hv["lo"][:, j, h, :]),
                            (P[s]["hi"][:, j, :], P[s]["lo"][:, j, :]), j == 0, j == NBLK - 1, "att0")
                P_free[s] = [(t,)] * NBLK
                t_att = t
                if h < 3:
                    t_P = build_P(s, h + 1, maskT["ne"], t_E, row)
                wait("act", t_att, *rowt_free[s])
                t = emit("act", lambda e, bk=bk: e.copy(rowt[s][0:66, :], bank[bk][0:66, :]), "yT", ns=520)
                bank_free[bk] = (t,)
                wait("pe", t)
                bk = take_bank(s)
                for i in range(NBLK):
                    t = emit("pe", lambda e, bk=bk, i=i: e.transpose(
                        bank[bk][:, i * 66:(i + 1) * 66], rowt[s][0:66, i * 128:(i + 1) * 128], ident[0:66, 0:66]),
                        "yTT", ns=60)
                rowt_free[s] = (t,)
                ov = bank[bk][:, 0:264].rearrange("p (i n) -> p i n", n=66)
                wait("dve", t)
                t = emit("dve", lambda e, ov=ov, h=h: e.tensor_scalar(m["D"][:, h, :], ov[:, :, 64], TINY, None,
                                                                      ALU.max), "D", ns=66)
                wait("dve", t)
                t = emit("dve", lambda e, h=h: e.reciprocal(m["rD"][:, h, :], m["D"][:, h, :]), "rD", ns=70)
                rb = m["rD"][:, h, :].rearrange("p (i o) -> p i o", o=1).broadcast_to([128, NBLK, 64])
                y = X[s][0][:, h % 2, 0:256].rearrange("p (i n) -> p i n", n=64)
                ex = X[s][0][:, h % 2, 256:512].rearrange("p (i n) -> p i n", n=64)
                xh = x[:, :, h * 64:(h + 1) * 64]
                if h < 2:
                    wait("dve", *raw_free[s])
                wait("dve", t)
                t = emit("dve", lambda e, y=y, ov=ov, rb=rb: e.tensor_tensor(y, ov[:, :, 0:64], rb, ALU.mult),
                         "y0", ns=335)
                bank_free[bk] = (t,)
                wait("act", t)
                te = emit("act", lambda e, y=y, ex=ex: e.activation(ex, y, ACT.Exp), "e0", ns=307)
                wait("act", te)
                tr = emit("act", lambda e, y=y: e.activation(y, y, ACT.Relu), "e0", ns=307)
                wait("dve", tr)
                t = emit("dve", lambda e, y=y, ex=ex: e.scalar_tensor_tensor(ex, ex, 1.0, y, ALU.min, ALU.add), "m0",
                         ns=335)
                wait("dve", t)
                t = emit("dve", lambda e, ex=ex, xh=xh: e.scalar_tensor_tensor(xh, ex, -1.0, xh, ALU.add, ALU.add),
                         "x0b", ns=335)
            raw_free[s] = (t,)
            hw_free[s] = (t_att,)
            t_layer[0, b] = (t,)

        def layer1a(b):
            s, x, o = b % LANES, xs[b % XSLOTS], oT
            m = sm[s]
            ta, tb = X[s]
            for bl in range(NBLK):
                t = block_stats(s, x, bl, t_layer[0, b])
            t_h = layer_norm(s, x, t)
            wait("pe", *t_w["m1"])
            wait("act", t_bias)
            t_o1 = []
            for fo in range(4):
                bk = take_bank(s)
                cols = slice(fo * 128, (fo + 1) * 128)
                for k in range(2):
                    wait("pe", t_h[k])
                    tp = mm3(bank[bk][:, :], (WM1["hi"][:, k, cols], WM1["lo"][:, k, cols]),
                             (hT[s]["hi"][:, k, :], hT[s]["lo"][:, k, :]), k == 0, k == 1, "m1")
                st = X[s][fo // 2][:, fo % 2, :]
                wait("act", tp, *(raw_free[s] if fo < 2 else st_free_of[s][fo - 2]))
                t = emit("act", lambda e, bk=bk, fo=fo, st=st: e.activation(
                    st, bank[bk][:, :], ACT.Relu, bias=b1[:, fo:fo + 1]), "m1", ns=571)
                bank_free[bk] = (t,)
                wait("act", t, *oT_free)
                t = emit("act", lambda e, fo=fo, st=st: e.copy(o["hi"][:, fo, :], st), "o1hi", ns=520)
                wait("pool", t, *oT_free)
                t_o = emit("pool", lambda e, fo=fo, st=st: e.tensor_tensor(
                    o["lo"][:, fo, :], st, f32(o["hi"][:, fo, :]), ALU.subtract), "o1lo", ns=1225)
                t_o1.append(t_o)
                if fo == 1:
                    raw_free[s] = (t_o,)
                elif fo > 1:
                    st_free_of[s][fo - 2] = (t_o,)
            P_free[s] = [(tp,)] * NBLK
            wait("pe", *t_w["fc"])
            t_raw, _ = project_raw(s, o, WFC, t_o1, 256)
            t_c0, t_E = scores(s, t_raw, 0.2, 1)
            row = row_of(s, m["E"][:, 2, 0, :], t_c0)
            t_P = build_P(s, 0, None, t_E, row)
            hw = hws[s]
            t_c = weight_columns(m["E"][:, 0, 0, :], wdf[s]["hi"][:, :], wdf[s]["lo"][:, :], t_E, hw_free[s])
            t_hw = scale_split(s, t_E, hw, hw_free[s])

            def attend_f(fo):
                bk = take_bank(s)
                fc = slice((fo % 2) * 128, (fo % 2 + 1) * 128)
                for j in range(NBLK):
                    tt = mm3(bank[bk][:, :], (hw["hi"][:, j, fc], hw["lo"][:, j, fc]),
                             (P[s]["hi"][:, j, :], P[s]["lo"][:, j, :]), j == 0, j == NBLK - 1, "attf")
                return bk, tt

            def post_y(fo, f):
                bk, t_at = f
                q = fo % 2
                wait("dve", t_at, t_rr, *raw_free[s])
                ty = emit("dve", lambda e: e.tensor_tensor(ta[:, q, :], bank[bk][:, :], rrow[:, :], ALU.mult),
                          "yf", ns=602)
                bank_free[bk] = (ty,)
                wait("act", ty, *st_free_of[s][q])
                te = emit("act", lambda e: e.activation(tb[:, q, :], ta[:, q, :], ACT.Exp), "ef", ns=520)
                return ty, te

            def post_pair(fos, t_e, t_proj):
                pair = [(n, fo, ta[:, fo % 2, :], tb[:, fo % 2, :]) for n, fo in enumerate(fos)]
                t, tr = [None, None], [None, None]
                for n, fo, y, ex in pair:
                    wait("dve", t_e[n])
                    t[n] = emit("dve", lambda e, ex=ex: e.tensor_scalar(ex, ex, 1.0, None, ALU.min), "mf",
                                ns=d_ns(256))
                for n, fo, y, ex in pair:
                    wait("act", t[n])
                    t[n] = emit("act", lambda e, ex=ex: e.activation(ex, ex, ACT.Exp, bias=minus1[:, 0:1]),
                                "ef2", ns=613)
                for n, fo, y, ex in pair:
                    tr[n] = emit("dve", lambda e, y=y, fo=fo: e.scalar_tensor_tensor(
                        y, y, 0.0, f32(o["hi"][:, fo, :]), ALU.max, ALU.add), "gf", ns=602)
                for n, fo, y, ex in pair:
                    wait("pool", tr[n])
                    tr[n] = emit("pool", lambda e, fo=fo, y=y: e.tensor_tensor(
                        y, y, f32(o["lo"][:, fo, :]), ALU.add), "resf", ns=1225)
                for n, fo, y, ex in pair:
                    wait("dve", t[n], tr[n])
                    t[n] = emit("dve", lambda e, y=y, ex=ex: e.scalar_tensor_tensor(
                        y, ex, -1.0, y, ALU.add, ALU.add), "o2", ns=602)
                td = t[1]
                t_o2 = [None, None]
                for n, fo, y, ex in pair:
                    wait("act", t[n], t_proj)
                    t[n] = emit("act", lambda e, fo=fo, y=y: e.copy(o["hi"][:, fo, :], y), "o2hi", ns=520)
                for n, fo, y, ex in pair:
                    eng = ("dve", "pool")[n]
                    wait(eng, t[n], t_proj)
                    t_o2[n] = emit(eng, lambda e, fo=fo, y=y: e.tensor_tensor(
                        o["lo"][:, fo, :], y, f32(o["hi"][:, fo, :]), ALU.subtract), "o2lo", ns=(602, 1225)[n])
                raw_free[s] = tuple(t_o2)
                st_free_of[s] = [(td,), (td,)]
                return t_o2

            wait("pe", t_c)
            bk = take_bank(s)
            for j in range(NBLK):
                wait("pe", t_P[j])
                t = mm3(bank[bk][:, :], tuple(wdf[s][p][:, j:j + 1].broadcast_to([128, 128]) for p in PARTS2),
                        (P[s]["hi"][:, j, :], P[s]["lo"][:, j, :]), j == 0, j == NBLK - 1, "Df")
            rrow = rowt[s]
            wait("act", t, *rowt_free[s])
            t = emit("act", lambda e, bk=bk: e.copy(rrow[0:1, :], bank[bk][0:1, :]), "rrow", ns=520)
            bank_free[bk] = (t,)
            wait("pe", t)
            bk = take_bank(s)
            for i in range(NBLK):
                t = emit("pe", lambda e, bk=bk, i=i: e.transpose(
                    bank[bk][:, i:i + 1], rrow[0:1, i * 128:(i + 1) * 128], ident[0:1, 0:1]), "Df", ns=TR_NS)
            wait("dve", t)
            t_rd = emit("dve", lambda e, bk=bk: e.reciprocal(m["rD"][:, 0, :], bank[bk][:, 0:NBLK]), "rD", ns=130)
            bank_free[bk] = (t_rd,)
            bk, t = row_of(s, m["rD"][:, 0, :], t_rd)
            wait("act", t)
            t_rr = emit("act", lambda e, bk=bk: e.copy(rrow[:, :], bank[bk][:, :]), "rrow", ns=520)
            bank_free[bk] = (t_rr,)
            wait("pe", t_hw)
            f2, f3 = attend_f(2), attend_f(3)
            hw_free[s] = (f3[1],)
            te = [post_y(2, f2)[1], post_y(3, f3)[1]]
            t_hw, t_proj = project_scaled(s, o, WFC, t_E, hw, hw_free[s], slice(0, 256))
            t23 = post_pair((2, 3), te, t_proj)
            wait("pe", t_hw)
            f2, f3 = attend_f(0), attend_f(1)
            hw_free[s] = (f3[1],)
            P_free[s] = [(f3[1],)] * NBLK
            y2, y3 = post_y(0, f2), post_y(1, f3)
            rowt_free[s] = (y3[0],)
            t_layer["1a", b] = post_pair((0, 1), (y2[1], y3[1]), t_proj) + t23

        def layer1b(b):
            nonlocal oT_free, rT_free
            s, x, o = b % LANES, xs[b % XSLOTS], oT
            m = sm[s]
            ta, tb = X[s]
            tA, tB = blocks(ta), blocks(tb)
            wait("pe", *t_w["m2"])
            wait("act", t_bias)
            bks = [take_bank(s), take_bank(s)]
            for fo, k in ((0, 2), (0, 3), (1, 2), (1, 3), (0, 0), (1, 0), (0, 1), (1, 1)):
                cols = slice(fo * 128, (fo + 1) * 128)
                wait("pe", t_layer["1a", b][k])
                t_m = mm3(bank[bks[fo]][:, :], (WM2["hi"][:, k, cols], WM2["lo"][:, k, cols]),
                          (o["hi"][:, k, :], o["lo"][:, k, :]), k == 2, k == 1, "m2")
                if k == 1:
                    bks[fo] = (bks[fo], t_m)
            oT_free = (t_m,)
            t_os = []
            for fo, (bk, tp) in enumerate(bks):
                wait("act", tp, *raw_free[s])
                t = emit("act", lambda e, bk=bk, fo=fo: e.activation(
                    ta[:, fo, :], bank[bk][:, :], ACT.Relu, bias=b2[:, fo:fo + 1]), "m2", ns=571)
                bank_free[bk] = (t,)
                wait("act", t, *rT_free)
                t_hs = emit("act", lambda e, fo=fo: e.activation(
                    rT["hi"][:, fo, :], ta[:, fo, :], ACT.Copy, accum_out=m["hs"][:, fo:fo + 1]), "o3hi",
                    ns=571)
                eng = ("pool", "dve")[fo]
                wait(eng, t_hs, *rT_free)
                t_o = emit(eng, lambda e, fo=fo: e.tensor_tensor(
                    rT["lo"][:, fo, :], ta[:, fo, :], f32(rT["hi"][:, fo, :]), ALU.subtract), "o3lo",
                    ns=(1225, 602)[fo])
                t_os.append(t_o)
            raw_free[s] = tuple(t_os)
            t_S = column_sums(s, WHA, t_hs)

            def turn_back(bp):
                bk = take_bank(s)
                for bb in range(2):
                    for k in range(2):
                        out = bank[bk][:, bb * 256 + k * 128:bb * 256 + (k + 1) * 128]
                        cols = slice((2 * bp + bb) * 128, (2 * bp + bb + 1) * 128)
                        for p in PARTS2:
                            tr = emit("pe", lambda e, out=out, k=k, cols=cols, p=p,
                                      st=(bb == 0 and k == 0 and p == "hi"):
                                      e.matmul(out, rT[p][:, k, cols], identr[:, :], start=st,
                                               stop=(p == "lo"), skip_group_check=True),
                                      "r3" if (bb, k, p) == (1, 1, "lo") else None, ns=54)
                return bk, tr

            wait("pe", *t_os)
            bk, tr = turn_back(0)
            wait("act", tr, *rowt_free[s])
            t_row = emit("act", lambda e, bk=bk: e.copy(rowt[s][:, :], bank[bk][:, :]), "r3", ns=520)
            bank_free[bk] = (t_row,)
            ends, r3, t_y, t_x2 = {}, {}, {}, {}

            def start(i, bk, td):
                wait("act", td, *raw_free[s])
                t_y[i] = emit("act", lambda e: e.activation(
                    tA[:, i, :], bank[bk][:, 0:256], ACT.Copy, scale=m["rD"][:, 0, i:i + 1]), "yh", ns=400)
                t_bk = t_y[i]
                third(i - 2)
                second(i - 1)
                first(i)
                return (t_bk,)

            def first(i):
                wait("dve", t_y[i], t_S)
                t = emit("dve", lambda e: e.scalar_tensor_tensor(
                    tA[:, i, :], m["Sb"][:, :], empty["gt"][:, i:i + 1], tA[:, i, :], ALU.mult, ALU.add), "yh2",
                    ns=396)
                wait("act", t, *st_free_of[s][0], *st_free_of[s][1])
                t_y[i] = emit("act", lambda e: e.activation(tB[:, i, :], tA[:, i, :], ACT.Exp), "eh", ns=307)

            def second(i):
                if i < 0:
                    return
                wait("dve", t_y[i])
                t = emit("dve", lambda e: e.tensor_scalar(tB[:, i, :], tB[:, i, :], 1.0, None, ALU.min), "mh",
                         ns=200)
                wait("act", t)
                t_y[i] = emit("act", lambda e: e.activation(tB[:, i, :], tB[:, i, :], ACT.Exp,
                                                            bias=minus1[:, 0:1]), "eh2", ns=400)
                if i < 2:
                    r3v, t3 = rowt[s][:, i * 256:(i + 1) * 256], t_row
                else:
                    if 1 not in r3:
                        r3[1] = turn_back(1)
                    bk, t3 = r3[1]
                    r3v = bank[bk][:, (i - 2) * 256:(i - 1) * 256]
                wait("dve", t3)
                ends[i] = emit("dve", lambda e: e.scalar_tensor_tensor(
                    tA[:, i, :], tA[:, i, :], 0.0, r3v, ALU.max, ALU.add), "gh", ns=335)
                if i == 3:
                    bank_free[bk] = (ends[i],)

            def third(i):
                if i < 0:
                    return
                xb = x[:, i, :]
                wait("dve", ends[i], t_y[i])
                t = emit("dve", lambda e: e.scalar_tensor_tensor(
                    tA[:, i, :], tB[:, i, :], -1.0, tA[:, i, :], ALU.add, ALU.add), "gh2", ns=335)
                wait("dve", t)
                t = emit("dve", lambda e: e.scalar_tensor_tensor(
                    xb, tA[:, i, :], 0.0, xb, ALU.max, ALU.add), "xh", ns=335)
                t_x2[i] = t
                ends[i] = block_stats(s, x, i, (t,))

            wait("pe", *t_w["ha"])
            gat256(s, rT, WHA, (t_os[0], t_os[1]), 0.2, maskT["gt"], start)
            third(2)
            second(3)
            third(3)
            rT_free = (r3[1][1],)
            rowt_free[s] = (t_x2[1],)
            raw_free[s] = (t_x2[3],)
            st_free_of[s] = [(t_x2[3],), (t_x2[3],)]
            t_layer["1b", b] = ends[3]

        def layer2(b):
            s, x = b % LANES, xs[b % XSLOTS]
            m = sm[s]
            ta, tb = X[s]
            tA, tB = blocks(ta), blocks(tb)
            t_h = layer_norm(s, x, t_layer["1b", b])
            t_e, t_x2, ends = {}, {}, {}

            def start(i, bk, td):
                wait("act", td, *raw_free[s], *st_free_of[s][0], *st_free_of[s][1])
                emit("act", lambda e: e.activation(
                    tA[:, i, :], bank[bk][:, 0:256], ACT.Relu, scale=m["rD"][:, 0, i:i + 1]), "rl2", ns=358)
                t_e[i] = emit("act", lambda e: e.activation(
                    tB[:, i, :], bank[bk][:, 0:256], ACT.Exp, scale=m["rD"][:, 0, i:i + 1]), "e2", ns=358)
                if i:
                    finish(i - 1)
                return (t_e[i],)

            def finish(i):
                xb = x[:, i, :]
                wait("dve", t_e[i])
                t = emit("dve", lambda e: e.scalar_tensor_tensor(
                    tA[:, i, :], tB[:, i, :], 1.0, tA[:, i, :], ALU.min, ALU.add), "g2", ns=335)
                wait("dve", t)
                t_x2[i] = emit("dve", lambda e: e.scalar_tensor_tensor(
                    xb, tA[:, i, :], -1.0, xb, ALU.add, ALU.add), "x2", ns=335)
                ends[i] = block_stats(s, x, i, (t_x2[i],))

            wait("pe", *t_w["L2"])
            gat256(s, hT[s], W2, t_h, 0.2, maskT["self"], start)
            finish(3)
            raw_free[s] = (t_x2[3],)
            st_free_of[s] = [(t_x2[3],), (t_x2[3],)]
            t_layer[2, b] = ends[3]

        t_store = {}

        def layer3(b):
            s, x = b % LANES, xs[b % XSLOTS]
            m = sm[s]
            tA = blocks(X[s][0])
            t_h = layer_norm(s, x, t_layer[2, b])
            t_S = column_sums(s, W3, t_h[1])
            if b + LANES < B:
                entry(b + LANES)
            t_y = {}

            def start(i, bk, td):
                wait("act", td, *raw_free[s])
                t_y[i] = emit("act", lambda e: e.activation(
                    tA[:, i, :], bank[bk][:, 0:256], ACT.Copy, scale=m["rD"][:, 0, i:i + 1]), "y3", ns=400)
                if i:
                    finish(i - 1)
                return (t_y[i],)

            def finish(i):
                xb = x[:, i, :]
                wait("dve", t_y[i], t_S)
                t = emit("dve", lambda e: e.scalar_tensor_tensor(
                    tA[:, i, :], m["Sb"][:, :], empty["ne"][:, i:i + 1], tA[:, i, :], ALU.mult, ALU.add), "y32",
                    ns=396)
                wait("dve", t)
                t_y[i] = emit("dve", lambda e: e.scalar_tensor_tensor(
                    xb, tA[:, i, :], 0.0, xb, ALU.max, ALU.add), "x3", ns=335)

            wait("pe", *t_w["L3"])
            gat256(s, hT[s], W3, t_h, 0.01, maskT["ne"], start)
            finish(3)
            raw_free[s] = (t_y[3],)
            wait("sp", t_y[3])
            t_store[b] = emit("sp", lambda e: e.dma_start(o_v[b], x[:, :, :]), f"out{b % XSLOTS}", ns=3000, by=16)
            x_free[b % XSLOTS] = (t_store[b],)

        def entry(b):
            s, x = b % LANES, xs[b % XSLOTS]
            for bl in range(NBLK):
                t = block_stats(s, x, bl, (t_x[b],))
            t_layer["rs", b] = rstd(s, t)

        def load(b):
            if b < B:
                L.lane, L.rank = "X", b
                load_x(b)

        for b in range(1, LANES):
            load(b)
        for b in range(B):
            load(b + LANES)
            L.lane, L.rank = f"L{b % LANES}", b
            if b < LANES:
                entry(b)
            for stage in (layer0, layer1a, layer1b, layer2, layer3):
                stage(b)
        for b in range(max(0, B - XSLOTS), B):
            L.pending.setdefault(("end", "sp"), []).append(t_store[b])
        ends = L.pending.pop(("end", "sp"))
        idle_in = identr[:, :].rearrange("p (o n) -> p o n", o=1).broadcast_to([128, 4, 128])
        L.idle = lambda e: e.matmul(bank[7][:, :], identr[:, :], idle_in, start=True, stop=True)
        order = L.merge()
        L.pending[("end", "sp")] = ends

        block = ctx.enter_context(nc.Block())

        @block.sync
        def _(e):
            L.play("sp", order, e)

        @block.tensor
        def _(e):
            L.play("pe", order, e)

        @block.vector
        def _(e):
            L.play("dve", order, e)

        @block.scalar
        def _(e):
            L.play("act", order, e)

        @block.gpsimd
        def _(e):
            L.play("pool", order, e)


_INS = ["x", "adj", "L0_gnn_W", "L0_gnn_a", "L1_gnn_mlp1_w", "L1_gnn_mlp1_b", "L1_gnn_mlp2_w", "L1_gnn_mlp2_b",
        "L1_gnn_W_fc", "L1_gnn_a_fc", "L1_gnn_W_hand", "L1_gnn_a_hand", "L2_gnn_W", "L2_gnn_a", "L3_gnn_W",
        "L3_gnn_a"]


def kernel(**inputs):
    import numpy as _np
    import concourse.bacc as _bacc
    from concourse import mybir as _mybir
    from concourse.bass_utils import run_bass_kernel_spmd as _run

    nc = _bacc.Bacc("TRN2", target_bir_lowering=False, num_devices=1)
    arrays, args = {}, []
    for name in _INS:
        a = _np.ascontiguousarray(inputs[name])
        arrays[f"in_{name}_dram"] = a
        args.append(nc.dram_tensor(f"in_{name}_dram", a.shape, _mybir.dt.from_np(a.dtype), kind="ExternalInput").ap())
    args.append(nc.dram_tensor("out_0_dram", (B, N, F), F32, kind="ExternalOutput").ap())
    build(nc, *args)
    r = _run(nc, [arrays], core_ids=[0])
    return r.results[0]["out_0_dram"]
```
